# Optimizing a Trainium2 kernel written in Bass

```python
import numpy as np
import jax
import jax.numpy as jnp

def _softmax(x, axis=-1):
    return jax.nn.softmax(x, axis=axis)

def _gelu(x):
    return jax.nn.gelu(x, approximate=True)

def _silu(x):
    return jax.nn.silu(x)

def _sigmoid(x):
    return jax.nn.sigmoid(x)

def _layernorm(x, axis=-1, eps=1e-05):
    m = jnp.mean(x, axis=axis, keepdims=True)
    v = jnp.var(x, axis=axis, keepdims=True)
    return (x - m) / jnp.sqrt(v + eps)

def _scatter_add(tgt, idx, src, axis=0):
    return tgt.at[idx].add(src)

def _segment_sum(src, seg, n):
    return jax.ops.segment_sum(src, seg, n)
kernel_name = 'mk_sandwich_d1_jaxref_r4_057d17'

def setup_inputs(seed: int=0):
    np.random.seed(seed)
    _w = jnp.asarray

    def _L0_attn_setup():
        import jax, jax.numpy as jnp
        import numpy as np
        K_FACTOR = 0.5
        key = jax.random.key(seed)
        k1, k2, k3, k4 = jax.random.split(key, 4)
        B, S, H, I = (1, 512, 1024, 2752)
        x = jax.random.normal(k1, (B, S, H), dtype=jnp.float32)
        w_gate = jax.random.normal(k2, (I, H), dtype=jnp.float32) * 0.02
        w_up = jax.random.normal(k3, (I, H), dtype=jnp.float32) * 0.02
        w_down = jax.random.normal(k4, (H, I), dtype=jnp.float32) * 0.02
        return {'x': x, 'w_gate': w_gate, 'w_up': w_up, 'w_down': w_down}
    _L0_attn_in = _L0_attn_setup()

    def _L0_ffn_setup():
        import jax, jax.numpy as jnp
        import numpy as np
        GROUP = 64

        def dequantize(W_q, scale, zero):
            out, half = W_q.shape
            hi = W_q >> 4 & 15
            lo = W_q & 15
            w = jnp.stack([hi, lo], axis=-1).reshape(out, half * 2).astype(scale.dtype)
            w = w.reshape(out, -1, GROUP)
            w = (w - zero[:, :, None]) * scale[:, :, None]
            return w.reshape(out, half * 2)
        key = jax.random.key(seed)
        ks = jax.random.split(key, 10)
        hidden, inter = (1024, 2752)
        B, S = (4, 256)
        x = jax.random.normal(ks[0], (B, S, hidden), dtype=jnp.float32)
        gate_Wq = jax.random.randint(ks[1], (inter, hidden // 2), 0, 64, dtype=jnp.int32)
        up_Wq = jax.random.randint(ks[2], (inter, hidden // 2), 0, 64, dtype=jnp.int32)
        down_Wq = jax.random.randint(ks[3], (hidden, inter // 2), 0, 64, dtype=jnp.int32)
        gate_scale = jax.random.uniform(ks[4], (inter, hidden // GROUP)) * 0.01 + 0.0001
        gate_zero = jax.random.uniform(ks[5], (inter, hidden // GROUP)) * 15.0
        up_scale = jax.random.uniform(ks[6], (inter, hidden // GROUP)) * 0.01 + 0.0001
        up_zero = jax.random.uniform(ks[7], (inter, hidden // GROUP)) * 15.0
        down_scale = jax.random.uniform(ks[8], (hidden, inter // GROUP)) * 0.01 + 0.0001
        down_zero = jax.random.uniform(ks[9], (hidden, inter // GROUP)) * 15.0
        return {'x': x, 'gate_Wq': gate_Wq, 'up_Wq': up_Wq, 'down_Wq': down_Wq, 'gate_scale': gate_scale, 'gate_zero': gate_zero, 'up_scale': up_scale, 'up_zero': up_zero, 'down_scale': down_scale, 'down_zero': down_zero}
    _L0_ffn_in = _L0_ffn_setup()
    _d = {'L0_attn_x': _L0_attn_in['x'], 'L0_attn_w_gate': _L0_attn_in['w_gate'], 'L0_attn_w_up': _L0_attn_in['w_up'], 'L0_attn_w_down': _L0_attn_in['w_down'], 'L0_ffn_gate_Wq': _L0_ffn_in['gate_Wq'], 'L0_ffn_up_Wq': _L0_ffn_in['up_Wq'], 'L0_ffn_down_Wq': _L0_ffn_in['down_Wq'], 'L0_ffn_gate_scale': _L0_ffn_in['gate_scale'], 'L0_ffn_gate_zero': _L0_ffn_in['gate_zero'], 'L0_ffn_up_scale': _L0_ffn_in['up_scale'], 'L0_ffn_up_zero': _L0_ffn_in['up_zero'], 'L0_ffn_down_scale': _L0_ffn_in['down_scale'], 'L0_ffn_down_zero': _L0_ffn_in['down_zero']}
    _x0 = _d['L0_attn_x']
    _d['L0_attn_x'] = jax.random.normal(jax.random.fold_in(jax.random.key(seed), 1), (1, 2048, 1024), dtype=_x0.dtype)
    del _x0
    return _d

def reference(L0_attn_x, L0_attn_w_gate, L0_attn_w_up, L0_attn_w_down, L0_ffn_gate_Wq, L0_ffn_up_Wq, L0_ffn_down_Wq, L0_ffn_gate_scale, L0_ffn_gate_zero, L0_ffn_up_scale, L0_ffn_up_zero, L0_ffn_down_scale, L0_ffn_down_zero):

    def _L0_attn_ref(x, w_gate, w_up, w_down):
        import jax, jax.numpy as jnp
        import numpy as np
        K_FACTOR = 0.5
        s = jax.nn.silu(jnp.einsum('bsh,ih->bsi', x, w_gate))
        B, S, I = s.shape
        k = int(K_FACTOR * I)
        _, idx = jax.lax.top_k(-jnp.abs(s), k)
        flat = s.reshape(B * S, I)
        rows = jnp.arange(B * S)[:, None]
        flat = flat.at[rows, idx.reshape(B * S, k)].set(0.0)
        s = flat.reshape(B, S, I)
        s = s * jnp.einsum('bsh,ih->bsi', x, w_up)
        return jnp.einsum('bsi,hi->bsh', s, w_down)

    def _L0_ffn_ref(x, gate_Wq, up_Wq, down_Wq, gate_scale, gate_zero, up_scale, up_zero, down_scale, down_zero):
        import jax, jax.numpy as jnp
        import numpy as np
        GROUP = 64

        def dequantize(W_q, scale, zero):
            out, half = W_q.shape
            hi = W_q >> 4 & 15
            lo = W_q & 15
            w = jnp.stack([hi, lo], axis=-1).reshape(out, half * 2).astype(scale.dtype)
            w = w.reshape(out, -1, GROUP)
            w = (w - zero[:, :, None]) * scale[:, :, None]
            return w.reshape(out, half * 2)
        Wg = dequantize(gate_Wq, gate_scale, gate_zero)
        Wu = dequantize(up_Wq, up_scale, up_zero)
        Wd = dequantize(down_Wq, down_scale, down_zero)
        g = jnp.einsum('bsh,ih->bsi', x, Wg)
        u = jnp.einsum('bsh,ih->bsi', x, Wu)
        h = jax.nn.silu(g) * u
        return jnp.einsum('bsi,hi->bsh', h, Wd)
    x = L0_attn_x
    x = x + _layernorm(_L0_attn_ref(_layernorm(x, axis=-1), L0_attn_w_gate, L0_attn_w_up, L0_attn_w_down), axis=-1)
    x = x + _layernorm(_L0_ffn_ref(_layernorm(x, axis=-1), L0_ffn_gate_Wq, L0_ffn_up_Wq, L0_ffn_down_Wq, L0_ffn_gate_scale, L0_ffn_gate_zero, L0_ffn_up_scale, L0_ffn_up_zero, L0_ffn_down_scale, L0_ffn_down_zero), axis=-1)
    return x

_drawn_inputs = setup_inputs


def setup_inputs(seed=0):
    import zlib

    import numpy as np

    out = dict(_drawn_inputs(seed))
    spreads = {}
    factors = {}
    for name, (base, spread) in spreads.items():
        noise = np.random.default_rng([zlib.crc32(name.encode()), seed]).standard_normal(out[name].shape)
        drawn = base * np.exp(spread * noise) if base else spread * noise
        out[name] = jnp.asarray(drawn.astype(out[name].dtype))
    for name, factor in factors.items():
        out[name] = (out[name] * factor).astype(out[name].dtype)
    return out
```

```python
from contextlib import ExitStack

import concourse.bass as bass
from concourse import mybir

FP32 = mybir.dt.float32
FP16 = mybir.dt.float16
INT32 = mybir.dt.int32
U8 = mybir.dt.uint8
ALU = mybir.AluOpType
ACT = mybir.ActivationFunctionType
AX = mybir.AxisListType
RMAX = bass.bass_isa.ReduceOp.max

P = 128
TOKENS, D, I, GROUP = 2048, 1024, 2752, 64
NT = TOKENS // P
KB = D // P
NCH = 8
CW = I // NCH
JB = (I // 2 + P - 1) // P
IB = 2 * JB
PL = I // 2 - (JB - 1) * P
NU, UW = 8, D // 8
BT = 4
NB = NT // BT
KEEP_FROM = I // 2
EPS = 1e-5
TOP = 2.0 ** 14
XS = 2.0 ** 10
TINY = 2.0 ** -100
EXP_BITS, ABS_BITS = 0x7F800000, 0x7FFFFFFF
QB = 4 * P
NBITS = 31
AG, AU, AD, BG, BU, BD = range(6)


class Steps:

    def __init__(self, sem):
        self.sem, self.base, self.n = sem, 0, 0

    def add(self, instruction, by=1):
        instruction.then_inc(self.sem, by)
        self.n += by
        return self.base + self.n

    def enter(self, i, per):
        kept = (self.base, self.n, per)
        self.base, self.n = i * per + (self.base + self.n), 0
        return kept

    def leave(self, kept, rounds):
        base, n, per = kept
        assert self.n == per, (self.n, per)
        self.base, self.n = base, n + rounds * per


def build(nc, x_in, wg_a, wu_a, wd_a, qg, qu, qd, sg, zg, su, zu, sd, zd, out):
    ctx = ExitStack()
    with ctx:
        def sb(name, shape, dt):
            return ctx.enter_context(nc.sbuf_tensor(name, shape, dt))

        def sem(name):
            return ctx.enter_context(nc.semaphore(name))

        def dram(name, shape, dt):
            return nc.dram_tensor(name, shape, dt, kind="Internal").ap()

        s_dram = dram("s_dram", (NT, P, I), FP32)
        u_dram = dram("u_dram", (NT, P, I), FP32)
        h_dram = dram("h_dram", (NT, P, I), FP32)
        x1_dram = dram("x1_dram", (NT, P, D), FP32)
        first_dram = dram("first_dram", (6, P, 1), FP32)
        wd_dram = [dram(f"wd{n}_dram", (NU, P, 2 * IB * UW), FP16) for n in range(2)]
        wgu_dram = [dram(f"wgu{n}_dram", (NCH, P, 2 * KB * CW), FP16) for n in range(2)]

        TR = sb("transposed", [P, NT * 2 * KB * P], FP16)
        W = sb("weights", [P, 2, 2 * 2 * IB * UW], FP16)
        S = sb("rows", [P, BT, IB * P], FP32)
        A = sb("sort_rows", [P, 3, I], FP32)
        JUNK = sb("junk", [P, 2, I], U8)
        Y = sb("y_rows", [P, BT, D], FP32)
        ident = sb("ident", [P, P], FP32)
        bitf = sb("bit_values", [P, 32], FP32)
        bitn = sb("next_bits", [P, 32], INT32)
        mx = sb("maxima", [P, 24 + 6], FP32)
        gmx = sb("global_maxima", [P, 6], FP32)
        mul = sb("scales", [P, 6], FP32)
        un = sb("unscales", [P, 6], FP32)
        st = sb("stats", [P, 12], FP32)
        mv = sb("mean_var", [P, 2], FP32)
        rs = sb("rstd", [P, 2], FP32)
        cons = sb("constants", [P, 1], FP32)
        cand = sb("candidates", [P, 2], INT32)
        flip = sb("flips", [P, 2], INT32)
        cnt = sb("counts", [P, 2], FP32)
        hs = sb("h_scale", [P, 4], FP32)
        inv_a = sb("h_unscale_a", [P, NT], FP32)
        inv_b = sb("h_unscale_b", [P, BT], FP32)

        PS = ctx.enter_context(nc.psum_tensor("psum", [P, 8, 512], FP32))

        xT_a = TR[:, :].rearrange("p (t h k m) -> p t h k m", t=NT, h=2, k=KB)
        hT = TR[:, 0:BT * 2 * IB * P].rearrange("p (t h k m) -> p t h k m", t=BT, h=2, k=IB)
        XB = BT * 2 * IB * P
        xT_b = TR[:, XB:XB + BT * 2 * KB * P].rearrange("p (t h k m) -> p t h k m", t=BT, h=2, k=KB)

        GU, DU = 2 * KB * CW, 2 * IB * UW

        def w_gu(slot, half):
            return W[:, slot, half * GU:(half + 1) * GU].rearrange("p (h k n) -> p h k n", h=2, k=KB)

        wa = W[:, :, :].rearrange("p s n -> p (s n)")[:, 0:4 * GU].rearrange("p (c h n) -> p c h n", c=4, h=2)
        w_down = [W[:, s, :].rearrange("p (u h k n) -> p u h k n", u=2, h=2, k=IB) for s in range(2)]

        def tp(slot, n):
            return PS[:, 2 * slot:2 * slot + 2, :].rearrange("p b n -> p (b n)")[:, 0:n * P]

        def raw(slot, n):
            return S[:, slot, 0:n]

        stage = [Y[:, 2 * g:2 * g + 2, :].rearrange("p a n -> p (a n)")[:, 0:BT * CW]
                 .rearrange("p (u n) -> p u n", u=BT) for g in range(2)]

        consts_ready = sem("consts_ready")
        max_full = [sem(f"max_full{j}") for j in range(4)]
        max_read = sem("max_read")
        zs_full, zs_read = sem("zs_full"), sem("zs_read")
        ident_ready, keep_used = sem("ident_ready"), sem("keep_used")
        maxima_ready, global_ready, scales_ready = sem("maxima_ready"), sem("global_ready"), sem("scales_ready")
        x_full = [sem(f"x_full{s}") for s in range(2)]
        var_ready, rstd_ready = sem("var_ready"), sem("rstd_ready")
        xs_ready = sem("xs_ready")
        tp_done = [sem(f"tp_done{s}") for s in range(2)]
        hi_done = [sem(f"hi_done{s}") for s in range(2)]
        lo_done = [sem(f"lo_done{s}") for s in range(2)]
        raw_full = [sem(f"raw_full{j}") for j in range(2)]
        split_hi, split_lo = sem("split_hi"), sem("split_lo")
        bzs_full = sem("bzs_full")
        w_ready = sem("w_ready")
        u_hi, u_lo, u_stored = sem("unit_hi"), sem("unit_lo"), sem("unit_stored")
        mm_done = [sem(f"mm_done{b}") for b in range(4)]
        bank_free = [sem(f"bank_free{b}") for b in range(4)]
        stored = [sem(f"stored{g}") for g in range(2)]
        su_full = [sem(f"su_full{j}") for j in range(2)]
        abs_ready = sem("abs_ready")
        cand_ready, act_count = sem("cand_ready"), sem("act_count")
        keep_ready = sem("keep_ready")
        s_again, u_again = sem("s_again"), sem("u_again")
        kill_ready = sem("kill_ready")
        h_ready, h_stored = sem("h_ready"), sem("h_stored")
        row_full = [sem(f"row_full{t}") for t in range(BT)]
        w_full = [sem(f"w_full{s}") for s in range(2)]
        ln_read = sem("ln_read")
        x1_ready, x1_stored = sem("x1_ready"), sem("x1_stored")
        hb_ready = sem("hb_ready")
        out_ready, out_stored = sem("out_ready"), sem("out_stored")
        passed = {e.engine: sem(f"passed{n}") for n, e in
                  enumerate((nc.sync, nc.scalar, nc.vector, nc.gpsimd, nc.tensor))}
        dve_s, pool_s = sem("dve_steps"), sem("pool_steps")

        def alone(engine):
            engine.sem_inc(passed[engine.engine], 1)

        block = ctx.enter_context(nc.Block())

        G_UP = NCH * NB
        G_BLOCKS = 2 * NCH * NB
        G_PER = 4 + NCH + NCH + 4
        T_BLOCKS = NT // 2
        T_PER = (3 * BT + BT + 3 * BT) // 2
        TSIZE = [8, 8, IB - 16]

        def chunk_groups():
            return ((0, AG), (1, AG), (2, AU), (3, AU))

        @block.sync
        def _(sp):
            for m, (src, n) in enumerate(((wg_a, KB * CW), (wu_a, KB * CW), (wd_a, IB * UW))):
                for r in range(2):
                    for j in range(4):
                        if m or r:
                            sp.wait_ge(max_read, 8 * m + 4 * r + j - 3)
                        sp.dma_start(raw(j, n), src[4 * r + j]).then_inc(max_full[j], 16)
            for n, (z, s, rows, cols) in enumerate(((zg, sg, P, CW), (zu, su, P, CW), (zd, sd, 4 * NU, JB * UW))):
                if n:
                    sp.wait_ge(zs_read, n)
                sp.dma_start(A[0:rows, 0, 0:cols], z.rearrange("c g n -> (c g) n")).then_inc(zs_full, 16)
                sp.dma_start(A[0:rows, 1, 0:cols], s.rearrange("c g n -> (c g) n")).then_inc(zs_full, 16)
            with sp.Fori(0, NT // 2) as i:
                for s in range(2):
                    sp.wait_ge(xs_ready, i * 2 + (s + 1))
                    alone(sp)
                    sp.dma_start(Y[:, s, :], x_in[i * 2 + s]).then_inc(x_full[s], 16)
            for j in range(4):
                sp.wait_ge(max_read if j == 0 else split_lo, 24 if j == 0 else j)
                alone(sp)
                sp.dma_start(raw(0, KB * CW), wg_a[j]).then_inc(raw_full[0], 16)
            for ph in range(4):
                with sp.Fori(0, 4) as i:
                    if ph < 3:
                        sp.wait_ge(split_lo, i + 4 * (ph + 1))
                        alone(sp)
                        src, off = (wg_a, 4) if ph == 0 else (wu_a, 4 * (ph - 1))
                        sp.dma_start(raw(0, KB * CW), src[i + off]).then_inc(raw_full[0], 16)
                    c = i + 4 * (ph % 2)
                    for k in range(2):
                        n = i * 2 + (8 * ph + k)
                        sp.wait_ge(u_lo, n + 1)
                        alone(sp)
                        if ph < 2:
                            q, z, s, rep, width = ((qg, zg, sg), (qu, zu, su))[k] + (KB, CW)
                            sp.dma_start(raw(1, KB // 2 * CW).bitcast(INT32), q[c]).then_inc(raw_full[0 + 1], 16)
                        elif k == 0:
                            sp.dma_start(raw(1, IB * UW), wd_a[c]).then_inc(raw_full[1], 16)
                            continue
                        else:
                            q, z, s, rep, width = qd, zd, sd, 32, JB * UW
                            sp.dma_start(raw(1, JB * UW).bitcast(INT32), q[c]).then_inc(raw_full[1], 16)
                        for d, a in ((0, z), (1, s)):
                            sp.dma_start(A[:, d, 0:width], a[c].unsqueeze(1).to_broadcast([P // rep, rep, width]))\
                                .then_inc(bzs_full, 16)
            sp.wait_ge(u_lo, 33)
            with sp.Fori(0, NT // 2) as i:
                for k in range(2):
                    sp.wait_ge(h_ready, i * 2 + 2)
                    alone(sp)
                    sp.wait_ge(stored[0], 32 * 16 + 16)
                    sp.wait_ge(stored[1], 32 * 16 + 16)
                    alone(sp)
                    sp.dma_start(A[:, k, :], s_dram[i * 2 + k]).then_inc(su_full[k], 16)
                for k in range(2):
                    sp.wait_ge(kill_ready, i * 2 + (k + 1))
                    alone(sp)
                    sp.dma_start(A[:, 2, :], s_dram[i * 2 + k]).then_inc(s_again, 16)
                    sp.wait_ge(keep_used, i * 2 + (k + 1))
                    alone(sp)
                    sp.dma_start(A[:, k, :], u_dram[i * 2 + k]).then_inc(u_again, 16)
            with sp.Fori(0, NB) as b:
                def load_w(n):
                    slot = n % 2
                    last = n - 2
                    if last < 0:
                        g = last
                    elif last < 4:
                        g = last
                    elif last < 12:
                        g = 5 + 2 * (last - 4)
                    else:
                        g = 8 + last
                    sp.wait_ge(mm_done[3], b * G_PER + (G_BLOCKS + g + 1))
                    alone(sp)
                    if n < 4 or n >= 12:
                        src = wd_dram[n // 12]
                        sp.dma_start(W[:, slot, :].rearrange("p (u n) -> p u n", u=2),
                                     src[2 * (n % 4):2 * (n % 4) + 2].rearrange("u p n -> p u n"))\
                            .then_inc(w_full[slot], 16)
                    else:
                        src = wgu_dram[(n - 4) // 4]
                        sp.dma_start(W[:, slot, 0:2 * GU].rearrange("p (u n) -> p u n", u=2),
                                     src[2 * (n % 4):2 * (n % 4) + 2].rearrange("u p n -> p u n"))\
                            .then_inc(w_full[slot], 16)
                if True:
                    sp.wait_ge(u_stored, 33 * 16)
                for t in range(BT):
                    sp.wait_ge(out_ready, b * BT + (t + 1))
                    alone(sp)
                    sp.wait_ge(h_stored, b * (BT * 16) + 16 * (t + 2))
                    alone(sp)
                    sp.dma_start(S[:, t, 0:I], h_dram[b * BT + t]).then_inc(row_full[t], 16)
                load_w(0)
                load_w(1)
                for t in range(BT):
                    g = 3 * t + 2
                    sp.wait_ge(tp_done[g % 2], b * T_PER + (T_BLOCKS + g // 2 + 1))
                    alone(sp)
                    sp.dma_start(S[:, t, 0:D], x_in[b * BT + t]).then_inc(row_full[t], 16)
                for n in range(2, 16):
                    load_w(n)
                for t in range(BT):
                    g = 4 * BT + 3 * t + 2
                    sp.wait_ge(tp_done[g % 2], b * T_PER + (T_BLOCKS + g // 2 + 1))
                    alone(sp)
                    sp.wait_ge(x1_stored, b * (BT * 16) + 16 * (t + 2))
                    alone(sp)
                    sp.dma_start(S[:, t, 0:D], x1_dram[b * BT + t]).then_inc(row_full[t], 16)

        @block.gpsimd
        def _(pool):
            nc.gpsimd.memset(ident[:, :], 0.0).then_inc(pool_s, 1)
            pool.wait_ge(pool_s, 1)
            nc.gpsimd.affine_select(out=ident[:, :], in_=ident[:, :], compare_op=ALU.not_equal, fill=1.0, base=0,
                                    pattern=[[-1, P]], channel_multiplier=1).then_inc(ident_ready, 1)
            nc.gpsimd.memset(cons[:, :], -0.5).then_inc(pool_s, 1)
            pool.wait_ge(ident_ready, 1)
            for n, done in enumerate((u_stored, stored[0], stored[1], h_stored, x1_stored, out_stored)):
                pool.dma_start(first_dram[n], ident[:, 0:1]).then_inc(done, 16)
            pool.wait_ge(maxima_ready, 6)
            nc.gpsimd.partition_all_reduce(gmx[:, :], mx[:, 24:30], P, RMAX).then_inc(global_ready, 1)
            pool.wait_ge(pool_s, 2)

            def rstd(n):
                pool.wait_ge(var_ready, n + 1)
                nc.gpsimd.tensor_tensor(rs[:, 0:1], mv[:, 1:2], cons[:, :], ALU.pow).then_inc(rstd_ready, 1)

            with pool.Fori(0, NT) as i:
                rstd(i)
            for ph in range(4):
                dst = s_dram if ph < 2 else u_dram
                with pool.Fori(0, 4) as i:
                    r = i + 4 * ph
                    c = i + 4 * (ph % 2)
                    for tp_ in range(2):
                        for g2 in range(2):
                            tq = 2 * tp_ + g2
                            pool.wait_ge(bank_free[3], r * 4 + (tq + 2))
                            alone(pool)
                            pool.dma_start(dst[4 * tq:4 * tq + 4, :, :].rearrange("t p (c n) -> p t c n", c=NCH)[:, :, c, :],
                                           stage[g2]).then_inc(stored[g2], 16)
                        n = r * 2 + tp_
                        pool.wait_ge(u_lo, n + 2)
                        alone(pool)
                        to = (wgu_dram[tp_] if ph < 2 else wd_dram[tp_])[c]
                        pool.dma_start(to, raw(2, to.shape[-1] // 2).bitcast(FP16)).then_inc(u_stored, 16)
            with pool.Fori(0, NT) as i:
                pool.wait_ge(h_ready, i + 3)
                alone(pool)
                pool.dma_start(h_dram[i], A[:, 2, :]).then_inc(h_stored, 16)
            with pool.Fori(0, NB) as b:
                for t in range(BT):
                    rstd(b * (3 * BT) + (NT + 2 * t))
                    pool.wait_ge(x1_ready, b * BT + (t + 1))
                    alone(pool)
                    pool.dma_start(x1_dram[b * BT + t], Y[:, t, :]).then_inc(x1_stored, 16)
                    rstd(b * (3 * BT) + (NT + 2 * t + 1))
                for t in range(BT):
                    rstd(b * (3 * BT) + (NT + 2 * BT + t))
                    pool.wait_ge(out_ready, b * BT + (BT + t + 1))
                    alone(pool)
                    pool.dma_start(out[b * BT + t], Y[:, t, :]).then_inc(out_stored, 16)
            pool.wait_ge(out_stored, 16 * (NT + 1))

        @block.scalar
        def _(act):
            for b_ in range(4):
                act.sem_inc(bank_free[b_], 1)

            def high(slot, use, dst, n):
                act.wait_ge(tp_done[slot], use + 1)
                alone(act)
                nc.scalar.activation(dst, tp(slot, n), ACT.Copy).then_inc(hi_done[slot], 1)

            with act.Fori(0, NT // 2) as i:
                for s in range(2):
                    high(s, i, xT_a[:, i * 2 + s, 0, :, :].rearrange("p k m -> p (k m)"), KB)

            def split_high(n, slot, m):
                act.wait_ge(raw_full[0], n * 16 + 16)
                alone(act)
                nc.scalar.activation(wa[:, slot, 0, :], raw(0, KB * CW), ACT.Copy, scale=mul[:, m:m + 1])\
                    .then_inc(split_hi, 1)

            act.wait_ge(scales_ready, 1)
            for j in range(4):
                split_high(j, j, AG)
            for ph in range(4):
                m = AG if ph < 2 else AU
                with act.Fori(0, 4) as i:
                    r = i + 4 * ph
                    for tp_ in range(2):
                        for g2 in range(2):
                            tq = 2 * tp_ + g2
                            act.wait_ge(stored[g2], r * 32 + (16 * (tp_ + 1)))
                            for u in range(4):
                                act.wait_ge(mm_done[u], r * 4 + (tq + 1))
                                nc.scalar.activation(stage[g2][:, u, :], PS[:, 4 + u, 0:CW],
                                                     ACT.Silu if ph < 2 else ACT.Copy, scale=un[:, m:m + 1])\
                                    .then_inc(bank_free[u], 1)
                        n = r * 2 + tp_
                        if ph < 2:
                            width, mi, w_src = KB * CW, (BG, BU)[tp_], raw(3, KB * CW)
                            act.wait_ge(w_ready, n + 1)
                        elif tp_ == 0:
                            width, mi, w_src = IB * UW, AD, raw(1, IB * UW)
                            act.wait_ge(raw_full[1], n * 16 + 16)
                        else:
                            width, mi, w_src = IB * UW, BD, raw(3, IB * UW)
                            act.wait_ge(w_ready, i + (16 + 4 * (ph - 2) + 1))
                        act.wait_ge(u_stored, n * 16 + 16)
                        nc.scalar.activation(raw(2, width).bitcast(FP16)[:, 0:width], w_src, ACT.Copy,
                                             scale=mul[:, mi:mi + 1]).then_inc(u_hi, 1)
                    if ph < 3:
                        split_high(r + 4, i, AG if ph == 0 else AU)
            with act.Fori(0, NT // 2) as i:
                with act.Fori(0, NBITS) as j:
                    act.wait_ge(cand_ready, i * (NBITS + 1) + j + 1)
                    nc.scalar.activation(JUNK[:, 1, :], A[:, 1, :], ACT.Sign, scale=-1.0,
                                         bias=cand[:, 1:2].bitcast(FP32), accum_out=cnt[:, 1:2]).then_inc(act_count, 1)
            with act.Fori(0, NB) as b:
                def group(g):
                    return b * G_PER + (G_BLOCKS + g)

                def use(g):
                    return b * T_PER + (T_BLOCKS + g // 2)

                def h_high(g0):
                    for t in range(BT):
                        for part in range(3):
                            g, n = g0 + 3 * t + part, TSIZE[part]
                            high(g % 2, use(g), hT[:, t, 0, 8 * part:8 * part + n, :].rearrange("p k m -> p (k m)"), n)

                def down_rows(g0, scale):
                    for c in range(4):
                        for t in range(BT):
                            act.wait_ge(mm_done[t], group(g0 + c) + 1)
                            alone(act)
                            nc.scalar.activation(Y[:, t, 2 * UW * c:2 * UW * (c + 1)], PS[:, 4 + t, 0:2 * UW],
                                                 ACT.Copy, scale=scale(t)).then_inc(bank_free[t], 1)

                h_high(0)
                act.wait_ge(out_stored, b * (BT * 16) + 16)
                down_rows(0, lambda t: inv_a[:, bass.ds(b * BT + t, 1)])
                for t in range(BT):
                    g = 3 * BT + t
                    high(g % 2, use(g), xT_b[:, t, 0, :, :].rearrange("p k m -> p (k m)"), KB)
                for c in range(NCH):
                    for t in range(BT):
                        act.wait_ge(mm_done[t], group(4 + c) + 1)
                        nc.scalar.activation(S[:, t, c * CW:(c + 1) * CW], PS[:, 4 + t, 0:CW], ACT.Silu,
                                             scale=un[:, BG:BG + 1]).then_inc(bank_free[t], 1)
                h_high(4 * BT)
                act.wait_ge(x1_stored, b * (BT * 16) + 16 * (BT + 1))
                down_rows(4 + 2 * NCH, lambda t: inv_b[:, t:t + 1])

        @block.vector
        def _(dve):
            step = Steps(dve_s)

            def then(ins, apart=False):
                value = step.add(ins)
                dve.wait_ge(dve_s, value)
                if apart:
                    alone(dve)

            dve.sem_inc(xs_ready, 2)
            dve.sem_inc(u_lo, 1)
            dve.sem_inc(lo_done[0], 1)
            dve.sem_inc(lo_done[1], 1)
            dve.sem_inc(h_ready, 2)
            dve.sem_inc(out_ready, BT)
            for j in range(NBITS):
                nc.vector.memset(bitf[:, j:j + 1], float(2 ** (NBITS - 1 - j)))
                last = nc.vector.memset(bitn[:, j:j + 1], 2 ** (NBITS - 2 - j) if j < NBITS - 1 else 0)
            then(last)
            then(nc.vector.memset(mx[:, :], 0.0))
            for m, n in enumerate((KB * CW, KB * CW, IB * UW)):
                for r in range(2):
                    for j in range(4):
                        dve.wait_ge(max_full[j], 16 * (2 * m + r + 1))
                        at = 8 * m + 4 * r + j
                        nc.vector.tensor_reduce(out=mx[:, at:at + 1], in_=raw(j, n), op=ALU.max, axis=AX.X,
                                                apply_absolute_value=True).then_inc(max_read, 1)
            for n, (rows, cols) in enumerate(((P, CW), (P, CW), (4 * NU, JB * UW))):
                z, s = A[0:rows, 0, 0:cols], A[0:rows, 1, 0:cols]
                dve.wait_ge(zs_full, 32 * (n + 1))
                then(nc.vector.tensor_scalar(z.bitcast(INT32), z.bitcast(INT32), ABS_BITS, None, ALU.bitwise_and))
                then(nc.vector.scalar_tensor_tensor(out=z, in0=z, scalar=15.0, in1=s, op0=ALU.add, op1=ALU.mult))
                nc.vector.tensor_reduce(out=mx[0:rows, 27 + n:28 + n], in_=z, op=ALU.max, axis=AX.X,
                                        apply_absolute_value=True).then_inc(zs_read, 1)
            dve.wait_ge(zs_read, 3)
            dve.wait_ge(max_read, 24)
            for m in range(3):
                nc.vector.tensor_reduce(out=mx[:, 24 + m:25 + m], in_=mx[:, 8 * m:8 * m + 8], op=ALU.max, axis=AX.X)\
                    .then_inc(maxima_ready, 2)
            dve.wait_ge(global_ready, 1)
            then(nc.vector.tensor_scalar(gmx[:, :], gmx[:, :], TINY, None, ALU.max))
            then(nc.vector.tensor_scalar(gmx[:, :].bitcast(INT32), gmx[:, :].bitcast(INT32), EXP_BITS, None,
                                         ALU.bitwise_and))
            then(nc.vector.reciprocal(mul[:, :], gmx[:, :]))
            then(nc.vector.tensor_scalar(mul[:, :], mul[:, :], TOP, None, ALU.mult))
            then(nc.vector.tensor_scalar(un[:, :], gmx[:, :], 1.0 / TOP, None, ALU.mult))
            for m in (AG, AU, BG, BU):
                then(nc.vector.tensor_scalar(un[:, m:m + 1], un[:, m:m + 1], 1.0 / XS, None, ALU.mult))
            nc.vector.memset(hs[:, :], 0.0).then_inc(scales_ready, 1)

            def mean_rstd(rows, n):
                half = D // 2
                nc.vector.bn_stats(st[:, 0:6], rows[:, 0:half])
                then(nc.vector.bn_stats(st[:, 6:12], rows[:, half:D]), apart=True)
                then(nc.vector.bn_aggr(mv[:, :], st[:, :]))
                nc.vector.tensor_scalar(mv[:, 1:2], mv[:, 1:2], EPS, None, ALU.add).then_inc(var_ready, 1)
                dve.wait_ge(rstd_ready, n + 1)

            def low(slot, use, dst, hi, n):
                dve.wait_ge(hi_done[slot], use + 1)
                nc.vector.tensor_tensor(dst, tp(slot, n), hi, ALU.subtract).then_inc(lo_done[slot], 1)

            def normalise_scaled(dst, rows):
                then(nc.vector.tensor_scalar(rs[:, 1:2], rs[:, 0:1], XS, None, ALU.mult))
                nc.vector.tensor_scalar(dst, rows, mv[:, 0:1], rs[:, 1:2], ALU.subtract, ALU.mult)\
                    .then_inc(xs_ready, 1)

            def flat(ap):
                return ap.rearrange("p k m -> p (k m)")

            with dve.Fori(0, NT // 2) as i:
                kept = step.enter(i, 6)
                for s in range(2):
                    dve.wait_ge(x_full[s], i * 16 + 16)
                    mean_rstd(Y[:, s, :], i * 2 + s)
                    dve.wait_ge(lo_done[s], i + 1)
                    normalise_scaled(Y[:, 2 + s, :], Y[:, s, :])
                    low(s, i, flat(xT_a[:, i * 2 + s, 1, :, :]), flat(xT_a[:, i * 2 + s, 0, :, :]), KB)
                step.leave(kept, NT // 2)

            def split_low(n, slot, m):
                dve.wait_ge(split_hi, n + 1)
                nc.vector.scalar_tensor_tensor(out=wa[:, slot, 1, :], in0=raw(0, KB * CW), scalar=mul[:, m:m + 1],
                                               in1=wa[:, slot, 0, :], op0=ALU.mult, op1=ALU.subtract)\
                    .then_inc(split_lo, 1)

            for j in range(4):
                split_low(j, j, AG)

            def dequantise(n_raw, n_zs, width, blocks):
                q = raw(1, blocks * width).bitcast(INT32).rearrange("p (j n) -> p j n", j=blocks)
                w = raw(3, 2 * blocks * width)
                wi = w.bitcast(INT32).rearrange("p (j e n) -> p j e n", j=blocks, e=2)
                dve.wait_ge(raw_full[1], n_raw * 16 + 16)
                nc.vector.tensor_scalar(wi[:, :, 0, :], q, 4, 15, ALU.logical_shift_right, ALU.bitwise_and)
                then(nc.vector.tensor_scalar(wi[:, :, 1, :], q, 15, None, ALU.bitwise_and))
                dve.wait_ge(bzs_full, n_zs * 32 + 32)
                return w

            with_units = [(0, 2), (1, 2), (2, 1), (3, 1)]
            for ph, _ in with_units:
                with dve.Fori(0, 4) as i:
                    r = i + 4 * ph
                    kept = step.enter(i, 4 if ph < 2 else 2)
                    for k in range(2):
                        n = r * 2 + k
                        dve.wait_ge(u_lo, n + 1)
                        if ph < 2:
                            mi, w = (BG, BU)[k], dequantise(n, n, CW, KB // 2)
                            w3 = w.rearrange("p (k n) -> p k n", k=KB)
                            wi3 = w.bitcast(INT32).rearrange("p (k n) -> p k n", k=KB)
                            z3 = A[:, 0, 0:CW].unsqueeze(1).to_broadcast([P, KB, CW])
                            s3 = A[:, 1, 0:CW].unsqueeze(1).to_broadcast([P, KB, CW])
                        elif k == 0:
                            mi, w = AD, raw(1, IB * UW)
                        else:
                            mi, w = BD, dequantise(n, i + (16 + 4 * (ph - 2)), UW, JB)
                            w3 = w.rearrange("p (j e n) -> p j e n", j=JB, e=2)
                            wi3 = w.bitcast(INT32).rearrange("p (j e n) -> p j e n", j=JB, e=2)
                            z3 = A[:, 0, 0:JB * UW].rearrange("p (j n) -> p j n", j=JB).unsqueeze(2)\
                                .to_broadcast([P, JB, 2, UW])
                            s3 = A[:, 1, 0:JB * UW].rearrange("p (j n) -> p j n", j=JB).unsqueeze(2)\
                                .to_broadcast([P, JB, 2, UW])
                        if ph < 2 or k:
                            then(nc.vector.tensor_tensor(w3, wi3, z3, ALU.subtract))
                            nc.vector.tensor_tensor(w3, w3, s3, ALU.mult).then_inc(w_ready, 1)
                        width = KB * CW if ph < 2 else IB * UW
                        hl = raw(2, width).bitcast(FP16)
                        dve.wait_ge(u_hi, n + 1)
                        nc.vector.scalar_tensor_tensor(out=hl[:, width:2 * width], in0=w, scalar=mul[:, mi:mi + 1],
                                                       in1=hl[:, 0:width], op0=ALU.mult, op1=ALU.subtract)\
                            .then_inc(u_lo, 1)
                    if ph < 3:
                        split_low(r + 4, i, AG if ph == 0 else AU)
                    step.leave(kept, 4)

            def h_scale(rows, inv, matrix):
                then(nc.vector.tensor_reduce(out=hs[:, 0:1], in_=rows, op=ALU.max, axis=AX.X, apply_absolute_value=True))
                then(nc.vector.tensor_scalar(hs[:, 0:1], hs[:, 0:1], TINY, None, ALU.max))
                then(nc.vector.tensor_scalar(hs[:, 1:2].bitcast(INT32), hs[:, 0:1].bitcast(INT32), EXP_BITS, None,
                                             ALU.bitwise_and))
                then(nc.vector.reciprocal(hs[:, 2:3], hs[:, 1:2]))
                then(nc.vector.tensor_scalar(hs[:, 2:3], hs[:, 2:3], TOP, None, ALU.mult))
                nc.vector.tensor_scalar(inv, hs[:, 1:2], 1.0 / TOP, un[:, matrix:matrix + 1], ALU.mult, ALU.mult)
                return nc.vector.tensor_scalar(rows, rows, hs[:, 2:3], None, ALU.mult)

            with dve.Fori(0, NT // 2) as i:
                kept = step.enter(i, 4 * NBITS + 2 * 14)
                for k in range(2):
                    dve.wait_ge(su_full[k], i * 16 + 16)
                    a = A[:, k, :].bitcast(INT32)
                    nc.vector.tensor_scalar(a, a, ABS_BITS, None, ALU.bitwise_and)
                nc.vector.memset(cand[:, :], 2 ** (NBITS - 1)).then_inc(cand_ready, 1)
                dve.wait_ge(cand_ready, i * (NBITS + 1) + 1)
                alone(dve)
                with dve.Fori(0, NBITS) as j:
                    bit = bitf[:, bass.ds(j, 1)]
                    nxt = bitn[:, bass.ds(j, 1)]
                    inner = step.enter(j, 4)
                    then(nc.vector.tensor_scalar(JUNK[:, 0, :], A[:, 0, :], cand[:, 0:1].bitcast(FP32), None,
                                                 ALU.is_lt, ALU.add, accum_out=cnt[:, 0:1]))
                    then(nc.vector.tensor_scalar(flip[:, 0:1], cnt[:, 0:1], KEEP_FROM - 0.5, bit, ALU.is_gt, ALU.mult))
                    dve.wait_ge(act_count, i * NBITS + j + 1)
                    then(nc.vector.tensor_scalar(flip[:, 1:2], cnt[:, 1:2], 0.0, bit, ALU.is_ge, ALU.mult))
                    then(nc.vector.tensor_tensor(cand[:, :], cand[:, :], flip[:, :], ALU.bitwise_xor))
                    nc.vector.tensor_tensor(cand[:, :], cand[:, :], nxt.to_broadcast([P, 2]), ALU.bitwise_xor)\
                        .then_inc(cand_ready, 1)
                    dve.wait_ge(cand_ready, i * (NBITS + 1) + j + 2)
                    step.leave(inner, NBITS)
                for k in range(2):
                    a, e = A[:, k, :], A[:, 2, :]
                    T = cand[:, k:k + 1]
                    Tf = T.bitcast(FP32)
                    then(nc.vector.tensor_scalar(JUNK[:, 0, :], a, Tf, None, ALU.is_le, ALU.add, accum_out=cnt[:, k:k + 1]))
                    then(nc.vector.tensor_scalar(flip[:, k:k + 1], cnt[:, k:k + 1], KEEP_FROM - 0.5, None, ALU.is_le),
                         apart=True)
                    then(nc.vector.tensor_tensor(T, T, flip[:, k:k + 1], ALU.add))
                    then(nc.vector.tensor_scalar(JUNK[:, 0, :], a, Tf, None, ALU.is_lt, ALU.add, accum_out=cnt[:, k:k + 1]))
                    then(nc.vector.tensor_scalar(cnt[:, k:k + 1], cnt[:, k:k + 1], -1.0, float(KEEP_FROM), ALU.mult, ALU.add))
                    then(nc.vector.tensor_scalar(JUNK[:, 0, :], a, Tf, None, ALU.is_equal))
                    dve.wait_ge(h_stored, i * 32 + (16 * (k + 1)))
                    then(nc.vector.tensor_tensor_scan(e, JUNK[:, 0, :], JUNK[:, 0, :], 0.0, ALU.add, ALU.bypass))
                    nc.vector.scalar_tensor_tensor(out=JUNK[:, 1, :], in0=e, scalar=cnt[:, k:k + 1],
                                                   in1=JUNK[:, 0, :], op0=ALU.is_le, op1=ALU.mult).then_inc(kill_ready, 1)
                    dve.wait_ge(kill_ready, i * 2 + (k + 1))
                    then(nc.vector.scalar_tensor_tensor(out=a, in0=a, scalar=Tf, in1=JUNK[:, 1, :],
                                                        op0=ALU.is_ge, op1=ALU.subtract))
                    dve.wait_ge(s_again, i * 32 + (16 * (k + 1)))
                    nc.vector.tensor_tensor(e, e, a, ALU.mult).then_inc(keep_used, 1)
                    dve.wait_ge(keep_used, i * 2 + (k + 1))
                    dve.wait_ge(u_again, i * 32 + (16 * (k + 1)))
                    then(nc.vector.tensor_tensor(e, e, a, ALU.mult))
                    h_scale(e, inv_a[:, bass.ds(i * 2 + k, 1)], AD).then_inc(h_ready, 1)
                step.leave(kept, NT // 2)

            with dve.Fori(0, NB) as b:
                kept = step.enter(b, BT * 14)

                def group(g):
                    return b * G_PER + (G_BLOCKS + g)

                def use(g):
                    return b * T_PER + (T_BLOCKS + g // 2)

                def h_low(g0):
                    for t in range(BT):
                        for part in range(3):
                            g, n = g0 + 3 * t + part, TSIZE[part]
                            low(g % 2, use(g), flat(hT[:, t, 1, 8 * part:8 * part + n, :]),
                                flat(hT[:, t, 0, 8 * part:8 * part + n, :]), n)

                h_low(0)
                for t in range(BT):
                    y = Y[:, t, :]
                    dve.wait_ge(bank_free[t], group(3) + 2)
                    n = b * (3 * BT) + (NT + 2 * t)
                    mean_rstd(y, n)
                    then(nc.vector.tensor_scalar(y, y, mv[:, 0:1], rs[:, 0:1], ALU.subtract, ALU.mult))
                    dve.wait_ge(row_full[t], b * 48 + 32)
                    nc.vector.tensor_tensor(y, y, S[:, t, 0:D], ALU.add).then_inc(x1_ready, 1)
                    dve.wait_ge(x1_ready, b * BT + (t + 1))
                    mean_rstd(y, n + 1)
                    normalise_scaled(S[:, t, D:2 * D], y)
                for t in range(BT):
                    g = 3 * BT + t
                    low(g % 2, use(g), flat(xT_b[:, t, 1, :, :]), flat(xT_b[:, t, 0, :, :]), KB)
                for c in range(NCH):
                    for t in range(BT):
                        dve.wait_ge(mm_done[t], group(4 + NCH + c) + 1)
                        rows = S[:, t, c * CW:(c + 1) * CW]
                        nc.vector.scalar_tensor_tensor(out=rows, in0=PS[:, 4 + t, 0:CW], scalar=un[:, BU:BU + 1],
                                                       in1=rows, op0=ALU.mult, op1=ALU.mult).then_inc(bank_free[t], 1)
                for t in range(BT):
                    dve.wait_ge(bank_free[t], group(4 + 2 * NCH - 1) + 2)
                    h_scale(S[:, t, 0:I], inv_b[:, t:t + 1], BD).then_inc(hb_ready, 1)
                h_low(4 * BT)
                for t in range(BT):
                    y = Y[:, t, :]
                    dve.wait_ge(bank_free[t], group(G_PER - 1) + 2)
                    mean_rstd(y, b * (3 * BT) + (NT + 2 * BT + t))
                    then(nc.vector.tensor_scalar(y, y, mv[:, 0:1], rs[:, 0:1], ALU.subtract, ALU.mult))
                    dve.wait_ge(row_full[t], b * 48 + 48)
                    nc.vector.tensor_tensor(y, y, S[:, t, 0:D], ALU.add).then_inc(out_ready, 1)
                step.leave(kept, NB)

        @block.tensor
        def _(pe):
            def transposes(slot, use, source, n):
                pe.wait_ge(lo_done[slot], use + 1)
                for k in range(n):
                    rows = source(k)
                    m = rows.shape[-1]
                    last = nc.tensor.transpose(tp(slot, n)[0:m, k * P:(k + 1) * P], rows, ident[:, :])
                last.then_inc(tp_done[slot], 1)

            def products(bank, lhs, rhs, blocks, width, rows_last=P):
                n = 0
                for kb in range(blocks):
                    m = rows_last if kb >= blocks - 2 else P
                    for hx, hw in ((0, 0), (0, 1), (1, 0)):
                        last = nc.tensor.matmul(PS[:, 4 + bank, 0:width], lhs(hx, kb, m), rhs(hw, kb, m),
                                                start=n == 0, stop=n == 3 * blocks - 1)
                        n += 1
                last.then_inc(mm_done[bank], 1)

            pe.wait_ge(ident_ready, 1)
            with pe.Fori(0, NT // 2) as i:
                for s in range(2):
                    rows = Y[:, 2 + s, :].rearrange("p (a k) -> p k a", k=KB)
                    pe.wait_ge(xs_ready, i * 2 + (s + 3))
                    transposes(s, i, lambda k: rows[:, k, :], KB)
            pe.wait_ge(lo_done[0], NT // 2 + 1)
            pe.wait_ge(lo_done[1], NT // 2 + 1)
            with pe.Fori(0, 4) as ph:
                with pe.Fori(0, 4) as i:
                    r = ph * 4 + i
                    pe.wait_ge(split_lo, r + 1)
                    alone(pe)
                    with pe.Fori(0, NT // 4) as tq:
                        for u in range(4):
                            pe.wait_ge(bank_free[u], r * 4 + tq + 1)
                            products(u, lambda h, kb, m: xT_a[:, tq * 4 + u, h, kb, :],
                                     lambda h, kb, m: wa[:, i, h, kb * CW:(kb + 1) * CW], KB, CW)
            with pe.Fori(0, NB) as b:
                def group(g):
                    return b * G_PER + (G_BLOCKS + g)

                def h_transposes(g0, ready):
                    for t in range(BT):
                        ready(t)
                        rows = S[:, t, :].rearrange("p (j m e) -> p j e m", j=JB, e=2)
                        for part in range(3):
                            g = g0 + 3 * t + part

                            def block_rows(k):
                                kb = 8 * part + k
                                return rows[:, kb // 2, kb % 2, 0:PL if kb >= IB - 2 else P]

                            transposes(g % 2, b * T_PER + (T_BLOCKS + g // 2), block_rows, TSIZE[part])
                    for s in range(2):
                        pe.wait_ge(lo_done[s], b * T_PER + (T_BLOCKS + (g0 + 3 * BT) // 2 + 1))

                def down(g0, n0):
                    for c in range(4):
                        slot = (n0 + c) % 2
                        pe.wait_ge(w_full[slot], b * 128 + 16 * ((n0 + c) // 2 + 1))
                        for t in range(BT):
                            pe.wait_ge(bank_free[t], group(g0 + c) + 1)
                            products(t, lambda h, kb, m: hT[0:m, t, h, kb, :],
                                     lambda h, kb, m: w_down[slot][0:m, :, h, kb, :], IB, 2 * UW, PL)

                def gate_up(g0, n0):
                    for c in range(NCH):
                        slot, half = (n0 + c // 2) % 2, c % 2
                        if half == 0:
                            pe.wait_ge(w_full[slot], b * 128 + 16 * ((n0 + c // 2) // 2 + 1))
                        for t in range(BT):
                            pe.wait_ge(bank_free[t], group(g0 + c) + 1)
                            products(t, lambda h, kb, m: xT_b[:, t, h, kb, :],
                                     lambda h, kb, m: w_gu(slot, half)[:, h, kb, :], KB, CW)

                h_transposes(0, lambda t: pe.wait_ge(row_full[t], b * 48 + 16))
                down(0, 0)
                for t in range(BT):
                    g = 3 * BT + t
                    pe.wait_ge(xs_ready, b * BT + (NT + 2 + t + 1))
                    rows = S[:, t, D:2 * D].rearrange("p (a k) -> p k a", k=KB)
                    transposes(g % 2, b * T_PER + (T_BLOCKS + g // 2), lambda k: rows[:, k, :], KB)
                for s in range(2):
                    pe.wait_ge(lo_done[s], b * T_PER + (T_BLOCKS + 2 * BT + 1))
                gate_up(4, 4)
                gate_up(4 + NCH, 8)
                h_transposes(4 * BT, lambda t: pe.wait_ge(hb_ready, b * BT + (t + 1)))
                down(4 + 2 * NCH, 12)


_NAMES = ["x", "wg_a", "wu_a", "wd_a", "qg", "qu", "qd", "sg", "zg", "su", "zu", "sd", "zd"]


def kernel(L0_attn_x, L0_attn_w_gate, L0_attn_w_up, L0_attn_w_down, L0_ffn_gate_Wq, L0_ffn_up_Wq, L0_ffn_down_Wq,
           L0_ffn_gate_scale, L0_ffn_gate_zero, L0_ffn_up_scale, L0_ffn_up_zero, L0_ffn_down_scale, L0_ffn_down_zero):
    import numpy as np
    import concourse.bacc as bacc
    from concourse.bass_utils import run_bass_kernel_spmd

    def contraction_chunks(w):
        w = np.asarray(w).T
        return w.reshape(P, w.shape[0] // P, NCH, CW).transpose(2, 0, 1, 3)

    def group_chunks(a):
        a = np.asarray(a).T
        return a.reshape(a.shape[0], NCH, CW).transpose(1, 0, 2)

    def padded(w, rows):
        w = np.asarray(w).T
        return np.concatenate([w, np.zeros((rows - w.shape[0], w.shape[1]), w.dtype)])

    def down_units(w):
        w = padded(w, IB * P).reshape(JB, P, 2, NU, UW)
        return w.transpose(3, 1, 0, 2, 4).reshape(NU, P, IB * UW)

    def packed_units(w):
        w = padded(w, JB * P).reshape(JB, P, NU, UW)
        return w.transpose(2, 1, 0, 3).reshape(NU, P, JB * UW)

    def group_units(a):
        a = padded(a, JB * 4).reshape(JB, 4, NU, UW)
        return a.transpose(2, 1, 0, 3).reshape(NU, 4, JB * UW)

    arrays = {
        "x": np.asarray(L0_attn_x).reshape(NT, P, D),
        "wg_a": contraction_chunks(L0_attn_w_gate).reshape(NCH, P, KB * CW),
        "wu_a": contraction_chunks(L0_attn_w_up).reshape(NCH, P, KB * CW),
        "wd_a": down_units(L0_attn_w_down),
        "qg": contraction_chunks(L0_ffn_gate_Wq).reshape(NCH, P, KB // 2 * CW),
        "qu": contraction_chunks(L0_ffn_up_Wq).reshape(NCH, P, KB // 2 * CW),
        "qd": packed_units(L0_ffn_down_Wq),
        "sg": group_chunks(L0_ffn_gate_scale), "zg": group_chunks(L0_ffn_gate_zero),
        "su": group_chunks(L0_ffn_up_scale), "zu": group_chunks(L0_ffn_up_zero),
        "sd": group_units(L0_ffn_down_scale), "zd": group_units(L0_ffn_down_zero),
    }
    arrays = {n: np.ascontiguousarray(a) for n, a in arrays.items()}
    nc = bacc.Bacc("TRN2", target_bir_lowering=False, num_devices=1)
    args = [nc.dram_tensor(f"in_{n}", arrays[n].shape, mybir.dt.from_np(arrays[n].dtype), kind="ExternalInput").ap()
            for n in _NAMES]
    out = nc.dram_tensor("out", (NT, P, D), FP32, kind="ExternalOutput").ap()
    build(nc, *args, out)
    r = run_bass_kernel_spmd(nc, [{f"in_{n}": arrays[n] for n in _NAMES}], core_ids=[0])
    return r.results[0]["out"].reshape(1, TOKENS, D)
```

```python
from contextlib import ExitStack

import concourse.bass as bass
from concourse import mybir

FP32 = mybir.dt.float32
FP16 = mybir.dt.float16
INT32 = mybir.dt.int32
U8 = mybir.dt.uint8
ALU = mybir.AluOpType
ACT = mybir.ActivationFunctionType
AX = mybir.AxisListType
RMAX = bass.bass_isa.ReduceOp.max

P = 128
TOKENS, D, I, GROUP = 2048, 1024, 2752, 64
NT = TOKENS // P
KB = D // P
NCH = 8
CW = I // NCH
JB = (I // 2 + P - 1) // P
IB = 2 * JB
PL = I // 2 - (JB - 1) * P
NU, UW = 8, D // 8
GU, DU = 2 * KB * CW, 2 * IB * UW
BT = 4
NB = NT // BT
DROPPED = I // 2
EPS = 1e-5
TOP = 2.0 ** 14
H_TOP = 2.0 ** 15
XS = 2.0 ** 10
TINY = 2.0 ** -100
EXP_BITS, ABS_BITS = 0x7F800000, 0x7FFFFFFF
NBITS = 31
AG, BG, BU, BD, AU, AD = range(6)
TPARTS = (8, 8, IB - 16)

UP_STEPS = ((2, 2, 2, 2), (2, 2, 2, 2), (2, 2, 2, 2), (2, 2, 2, 2))
DOWN_A_STEPS = (3, 7, 7, 0)
GATE_STEPS = (2, 3, 3, 3, 3, 0, 0, 0)
UP_B_STEPS = (2,) * 8
DOWN_B_STEPS = (0, 8, 7, 0)
SLOTS = 32


class Steps:

    def __init__(self, sem):
        self.sem, self.base, self.n = sem, 0, 0

    def add(self, instruction, by=1):
        instruction.then_inc(self.sem, by)
        self.n += by
        return self.base + self.n

    def enter(self, i, per):
        kept = (self.base, self.n, per)
        self.base, self.n = i * per + (self.base + self.n), 0
        return kept

    def leave(self, kept, rounds):
        base, n, per = kept
        assert self.n == per, (self.n, per)
        self.base, self.n = base, n + rounds * per


def build(nc, x_in, wg_a, wu_a, wd_a, qg, qu, qd, sg, zg, su, zu, sd, zd, out):
    ctx = ExitStack()
    with ctx:
        def sb(name, shape, dt):
            return ctx.enter_context(nc.sbuf_tensor(name, shape, dt))

        def sem(name):
            return ctx.enter_context(nc.semaphore(name))

        def sems(name, n):
            return [sem(f"{name}{j}") for j in range(n)]

        def dram(name, shape, dt):
            return nc.dram_tensor(name, shape, dt, kind="Internal").ap()

        s_dram = dram("s_dram", (NT, P, I), FP32)
        m_dram = dram("m_dram", (NT, P, I), FP32)
        u_dram = dram("u_dram", (NT, P, I), FP32)
        x1_dram = dram("x1_dram", (NT, P, D), FP32)
        first_dram = dram("first_dram", (7, P, 1), FP32)
        wd_dram = [dram(f"wd{n}_dram", (NU, P, DU), FP16) for n in range(2)]
        wgu_dram = [dram(f"wgu{n}_dram", (NCH, P, GU), FP16) for n in range(2)]

        TR = sb("transposed", [P, NT * 2 * KB * P], FP16)
        W = sb("weights", [P, 2, 2 * DU], FP16)
        S = sb("rows", [P, BT, IB * P], FP32)
        A = sb("search_rows", [P, 3 * I + 64], FP32)
        JUNK = sb("junk", [P, 2, I], U8)
        Y = sb("y_rows", [P, BT, D], FP32)
        ident = sb("ident", [P, P], FP32)
        bitf = sb("bit_values", [P, SLOTS], FP32)
        bitn = sb("next_bits", [P, SLOTS], INT32)
        mx = sb("maxima", [P, 24 + 6], FP32)
        gmx = sb("global_maxima", [P, 6], FP32)
        mul = sb("scales", [P, 6], FP32)
        un = sb("unscales", [P, 6], FP32)
        st = sb("stats", [P, BT, 12], FP32)
        mv = sb("mean_var", [P, BT, 2], FP32)
        rs = sb("rstd", [P, BT], FP32)
        rx = sb("rstd_scaled", [P, BT], FP32)
        half = sb("minus_half", [P, BT], FP32)
        cand = sb("candidates", [P, 2], INT32)
        flip = sb("flips", [P, 2], INT32)
        cnt = sb("counts", [P, 2], FP32)
        fin = sb("ranks_dropped", [P, 4], FP32)
        hmax = sb("h_maxima", [P, BT, NCH + 1], FP32)
        hs = sb("h_scales", [P, 2, BT], FP32)
        inv = sb("h_unscales", [P, 2, BT], FP32)
        PS = ctx.enter_context(nc.psum_tensor("psum", [P, 8, 512], FP32))

        xT_a = TR[:, :].rearrange("p (t h k m) -> p t h k m", t=NT, h=2, k=KB)
        HB, XB = BT * 2 * IB * P, BT * 2 * KB * P
        hT = TR[:, 0:HB].rearrange("p (t h k m) -> p t h k m", t=BT, h=2, k=IB)
        xT_b = TR[:, HB:HB + XB].rearrange("p (t h k m) -> p t h k m", t=BT, h=2, k=KB)
        x1_row = TR[:, HB + XB:HB + XB + 2 * D].bitcast(FP32)
        a_row = [A[:, k * I:(k + 1) * I] for k in range(3)]
        m_row = A[:, 2 * I:2 * I + IB * UW]
        x_half = [A[:, n * BT * D:(n + 1) * BT * D].rearrange("p (t n) -> p t n", t=BT) for n in range(2)]
        wa = W[:, :, :].rearrange("p s n -> p (s n)")[:, 0:4 * GU].rearrange("p (c h n) -> p c h n", c=4, h=2)
        w_down = [W[:, s, :].rearrange("p (u h k n) -> p u h k n", u=2, h=2, k=IB) for s in range(2)]
        w_f32 = W[:, :, :].rearrange("p s n -> p (s n)").bitcast(FP32)
        ZW = JB * UW
        bounds_in = [(w_f32[:, (2 * n) * ZW:(2 * n + 1) * ZW], w_f32[:, (2 * n + 1) * ZW:(2 * n + 2) * ZW])
                     for n in range(3)]

        def w_gu(slot, part):
            return W[:, slot, part * GU:(part + 1) * GU].rearrange("p (h k n) -> p h k n", h=2, k=KB)

        def tp(slot, n):
            return PS[:, 2 * slot:2 * slot + 2, :].rearrange("p b n -> p (b n)")[:, 0:n * P]

        def raw(slot, n):
            return S[:, slot, 0:n]

        def flat(ap):
            return ap.rearrange("p k m -> p (k m)")

        stage = [Y[:, 2 * g:2 * g + 2, :].rearrange("p a n -> p (a n)")[:, 0:BT * CW]
                 .rearrange("p (u n) -> p u n", u=BT) for g in range(2)]
        BOUNDS = ((zg, sg, P, CW), (zu, su, P, CW), (zd, sd, 4 * NU, ZW))
        UNITS = ((qg, zg, sg, KB, CW, BG), (qu, zu, su, KB, CW, BU), (qd, zd, sd, 32, ZW, BD))

        ident_ready = sem("ident_ready")
        zs_full, x_full = sem("zs_full"), sems("x_full", 4)
        max_full = sems("max_full", 4)
        max_next = sem("max_next")
        max_read = sem("max_read")
        maxima_ready, global_ready = sem("maxima_ready"), sem("global_ready")
        scales_ready = sem("scales_ready")
        var_ready, rstd_ready = sem("var_ready"), sem("rstd_ready")
        xs_ready = sem("xs_ready")
        tp_done = sems("tp_done", 2)
        hi_done = sems("hi_done", 2)
        lo_done = sems("lo_done", 2)
        chunk_full = sem("chunk_full")
        split_hi, split_lo = sem("split_hi"), sem("split_lo")
        unit_full, unit_zs = sem("unit_full"), sem("unit_zs")
        w_ready = sem("w_ready")
        u_hi, u_lo = sem("unit_hi"), sem("unit_lo")
        u_stored = sem("unit_stored")
        mm_done = sems("mm_done", BT)
        bank_free = sems("bank_free", BT)
        stored = sems("stored", 2)
        s_full = sems("s_full", 2)
        cand_ready = sems("cand_ready", 2)
        act_count = sems("act_count", 2)
        kill_ready, s_again = sem("kill_ready"), sem("s_again")
        m_ready, m_stored = sem("masked_ready"), sems("masked_stored", 2)
        u_full, u_read = sem("u_full"), sem("u_read")
        h_ready = sem("h_ready")
        row_full = sems("row_full", BT)
        x1_full = sem("x1_full")
        w_full = sems("w_full", 2)
        x1_ready, x1_stored = sem("x1_ready"), sem("x1_stored")
        hb_ready = sem("hb_ready")
        out_ready, out_stored = sem("out_ready"), sem("out_stored")
        dve_steps, pool_steps = sem("dve_steps"), sem("pool_steps")
        passed = {e.engine: sem(f"passed{n}") for n, e in
                  enumerate((nc.sync, nc.scalar, nc.vector, nc.gpsimd, nc.tensor))}

        def alone(engine):
            engine.sem_inc(passed[engine.engine], 1)

        block = ctx.enter_context(nc.Block())

        G_BLOCKS, G_PER = 2 * NCH * NB, 4 + NCH + NCH + 4
        G_GATE, G_UP, G_DOWN = 4, 4 + NCH, 4 + 2 * NCH
        T_BLOCKS, T_PER = NT // 2, (3 * BT + BT + 3 * BT) // 2
        T_X, T_H = 3 * BT, 4 * BT

        def group(b, g):
            return b * G_PER + (G_BLOCKS + g)

        def use(b, g):
            return b * T_PER + (T_BLOCKS + g // 2)

        def pair_base(b, pair, per, per_up):
            return per_up * pair if b is None else (b * 2 + pair) * per + 2 * per_up

        def for_blocks(engine, body):
            with engine.Fori(0, NB - 1) as b:
                body(b, True)
            body(NB - 1, False)

        @block.sync
        def _(sp):
            for n, (z, s, rows, cols) in enumerate(BOUNDS):
                for dst, src in zip(bounds_in[n], (z, s)):
                    sp.dma_start(dst[0:rows, 0:cols], src.rearrange("c g n -> (c g) n")).then_inc(zs_full, 16)

            def x_batch(n):
                if n >= 2:
                    for s in range(2):
                        sp.wait_ge(tp_done[s], 2 * (n - 1))
                sp.dma_start(x_half[n % 2], x_in[BT * n:BT * (n + 1)].rearrange("t p n -> p t n"))\
                    .then_inc(x_full[n], 16)

            x_batch(0)
            for j in range(4):
                sp.dma_start(raw(j, KB * CW), wg_a[4 + j]).then_inc(max_full[j], 16)
            x_batch(1)
            for j in range(4):
                sp.wait_ge(max_read, j + 1)
                sp.dma_start(raw(j, KB * CW), wg_a[j]).then_inc(max_full[j], 16)
            x_batch(2)
            x_batch(3)
            for s in range(2):
                sp.wait_ge(tp_done[s], NT // 2)
            sp.wait_ge(split_lo, 4)

            def chunk(i, ph):
                src, off = (wg_a, 4) if ph == 0 else (wu_a, 4 * (ph - 1))
                sp.wait_ge(split_lo, i + 4 * (ph + 1))
                alone(sp)
                sp.dma_start(raw(0, KB * CW), src[i + off]).then_inc(chunk_full, 16)

            def unit(n, src, c, width, zeros_scales=None):
                sp.wait_ge(u_lo, n + 1)
                alone(sp)
                dst = raw(1, width).bitcast(INT32) if zeros_scales else raw(1, width)
                sp.dma_start(dst, src[c]).then_inc(unit_full, 16)
                if zeros_scales:
                    z, s, rep, cols = zeros_scales
                    for k, a in ((0, z), (1, s)):
                        sp.dma_start(a_row[k][:, 0:cols], a[c].unsqueeze(1).to_broadcast([P // rep, rep, cols]))\
                            .then_inc(unit_zs, 16)

            def for_maximum(i, ph, k):
                src, n = (wu_a, KB * CW) if ph == 0 else (wd_a, IB * UW)
                sp.wait_ge(max_read, i * 2 + (8 * (ph + 1) + k))
                alone(sp)
                sp.dma_start(m_row[:, 0:n], src[i * 2 + k]).then_inc(max_next, 16)

            for ph in range(2):
                with sp.Fori(0, 4) as i:
                    chunk(i, ph)
                    for k, (q, z, s, rep, cols, _) in enumerate(UNITS):
                        if k != 1:
                            for_maximum(i, ph, k // 2)
                        unit(i * 3 + (12 * ph + k), q, i + 4 * ph, q.shape[-1], (z, s, rep, cols))

            def search_rows(first, first_stored):
                for k in range(2):
                    sp.wait_ge(m_stored[k], first_stored)
                    alone(sp)
                    sp.dma_start(a_row[k], s_dram[first + k]).then_inc(s_full[k], 16)

            def mask_rows(first):
                for k in range(2):
                    sp.wait_ge(kill_ready, first + (k + 1))
                    alone(sp)
                    sp.dma_start(a_row[2], s_dram[first + k]).then_inc(s_again, 16)

            for s in range(2):
                sp.wait_ge(stored[s], 16 * (NCH * NB // 2 + 1))
            sp.wait_ge(u_lo, 25)
            sp.wait_ge(max_read, 24)
            search_rows(0, 16)
            with sp.Fori(0, 4) as i:
                chunk(i, 2)
                unit(i + 24, wd_a, i, IB * UW)
            mask_rows(0)
            search_rows(2, 16 * 2)
            with sp.Fori(0, 4) as i:
                unit(i + 28, wd_a, i + 4, IB * UW)
            mask_rows(2)
            sp.wait_ge(u_stored, 16 * 33)
            for s in range(2):
                sp.wait_ge(stored[s], 16 * (NCH * NB + 1))
            for t in range(BT):
                sp.wait_ge(m_stored[t % 2], 16 * (t // 2 + 2))
                sp.dma_start(S[:, t, 0:I], m_dram[t]).then_inc(row_full[t], 16)
                if t:
                    sp.wait_ge(u_read, t)
                else:
                    sp.wait_ge(m_ready, BT)
                sp.dma_start(a_row[2], u_dram[t]).then_inc(u_full, 16)

            def blocks(b, search):
                def weights(*ns):
                    for n in ns:
                        last = n - 2
                        g = last if last < 4 else 5 + 2 * (last - 4) if last < 12 else 8 + last
                        sp.wait_ge(mm_done[BT - 1], group(b, g + 1))
                        alone(sp)
                        src = wd_dram[n // 12] if n < 4 or n >= 12 else wgu_dram[(n - 4) // 4]
                        size = src.shape[-1]
                        sp.dma_start(W[:, n % 2, 0:2 * size].rearrange("p (u n) -> p u n", u=2),
                                     src[2 * (n % 4):2 * (n % 4) + 2].rearrange("u p n -> p u n"))\
                            .then_inc(w_full[n % 2], 16)

                first = b * BT + BT
                weights(0, 1)
                if search:
                    search_rows(first, b * 32 + 48)
                for t in range(BT):
                    g = 3 * t + 2
                    sp.wait_ge(tp_done[g % 2], use(b, g) + 1)
                    alone(sp)
                    sp.dma_start(S[:, t, 0:D], x_in[b * BT + t]).then_inc(row_full[t], 16)
                weights(2, 3, 4, 5, 6, 7, 8)
                if search:
                    mask_rows(first)
                weights(9)
                if search:
                    search_rows(first + 2, b * 32 + 64)
                weights(10, 11, 12, 13)
                for t in range(BT):
                    if search:
                        if t == 2:
                            weights(14, 15)
                            mask_rows(first + 2)
                        g = T_H + 3 * t + 2
                        sp.wait_ge(tp_done[g % 2], use(b, g) + 1)
                        alone(sp)
                        sp.wait_ge(m_stored[t % 2], b * 32 + (16 * (t // 2) + 64))
                        alone(sp)
                        sp.dma_start(S[:, t, 0:I], m_dram[first + t]).then_inc(row_full[t], 16)
                        sp.wait_ge(u_read, first + t)
                        alone(sp)
                        if t % 2 == 0:
                            sp.wait_ge(m_ready, first + (t + 2))
                            alone(sp)
                        sp.dma_start(a_row[2], u_dram[first + t]).then_inc(u_full, 16)
                if not search:
                    weights(14, 15)
                for t in range(BT):
                    sp.wait_ge(x1_stored, b * (16 * BT) + 16 * (t + 2))
                    alone(sp)
                    sp.wait_ge(out_ready, b * BT + (t + 1))
                    alone(sp)
                    sp.dma_start(x1_row, x1_dram[b * BT + t]).then_inc(x1_full, 16)

            for_blocks(sp, blocks)

        @block.gpsimd
        def _(pool):
            nc.gpsimd.memset(ident[:, :], 0.0).then_inc(pool_steps, 1)
            nc.gpsimd.memset(half[:, :], -0.5).then_inc(pool_steps, 1)
            pool.wait_ge(pool_steps, 2)
            nc.gpsimd.affine_select(out=ident[:, :], in_=ident[:, :], compare_op=ALU.not_equal, fill=1.0, base=0,
                                    pattern=[[-1, P]], channel_multiplier=1).then_inc(ident_ready, 1)
            pool.wait_ge(ident_ready, 1)
            for n, done in enumerate((u_stored, *stored, *m_stored, x1_stored, out_stored)):
                pool.dma_start(first_dram[n], ident[:, 0:1]).then_inc(done, 16)

            def rstd(n, cols):
                pool.wait_ge(var_ready, n + 1)
                nc.gpsimd.tensor_tensor(rs[:, cols], mv[:, cols, 1], half[:, cols], ALU.pow).then_inc(rstd_ready, 1)

            def over_partitions(n, cols):
                pool.wait_ge(maxima_ready, n)
                nc.gpsimd.partition_all_reduce(gmx[:, cols], mx[:, 24 + cols.start:24 + cols.stop], P, RMAX)\
                    .then_inc(global_ready, 1)

            rstd(0, slice(0, BT))
            rstd(1, slice(0, BT))
            over_partitions(1, slice(0, 4))
            rstd(2, slice(0, BT))
            rstd(3, slice(0, BT))
            for ph in range(4):
                dst = s_dram if ph < 2 else u_dram
                with pool.Fori(0, 4) as i:
                    c = i + 4 * (ph % 2)
                    for tq in range(4):
                        pool.wait_ge(bank_free[BT - 1], i * 4 + (16 * ph + tq + 2))
                        alone(pool)
                        pool.dma_start(dst[BT * tq:BT * (tq + 1)].rearrange("t p (c n) -> p t c n", c=NCH)[:, :, c, :],
                                       stage[tq % 2]).then_inc(stored[tq % 2], 16)
                        if tq and (ph < 2 or tq == 1):
                            n, to = (i * 3 + (12 * ph + tq - 1), (*wgu_dram, wd_dram[1])[tq - 1]) if ph < 2 else \
                                (i + (24 + 4 * (ph - 2)), wd_dram[0])
                            pool.wait_ge(u_lo, n + 2)
                            alone(pool)
                            pool.dma_start(to[c], raw(2, to.shape[-1] // 2).bitcast(FP16)).then_inc(u_stored, 16)
                if ph < 2:
                    over_partitions(2 + ph, slice(4 + ph, 5 + ph))
                else:
                    for k in range(2):
                        t = 2 * (ph - 2) + k
                        pool.wait_ge(m_ready, t + 1)
                        pool.dma_start(m_dram[t], a_row[k]).then_inc(m_stored[k], 16)

            def masked(first):
                for k in range(2):
                    pool.wait_ge(m_ready, first + (k + 1))
                    alone(pool)
                    pool.dma_start(m_dram[first + k], a_row[k]).then_inc(m_stored[k], 16)

            def blocks(b, search):
                n = b * (3 * BT) + 4
                for t in range(BT):
                    rstd(n + 2 * t, slice(t, t + 1))
                    pool.wait_ge(x1_ready, b * BT + (t + 1))
                    alone(pool)
                    pool.dma_start(x1_dram[b * BT + t], Y[:, t, :]).then_inc(x1_stored, 16)
                    rstd(n + (2 * t + 1), slice(t, t + 1))
                if search:
                    masked(b * BT + BT)
                    masked(b * BT + (BT + 2))
                for t in range(BT):
                    rstd(n + (2 * BT + t), slice(t, t + 1))
                    pool.wait_ge(out_ready, b * BT + (t + 2))
                    alone(pool)
                    pool.dma_start(out[b * BT + t], Y[:, t, :]).then_inc(out_stored, 16)

            for_blocks(pool, blocks)
            pool.wait_ge(out_stored, 16 * (NT + 1))

        @block.scalar
        def _(act):
            for u in range(BT):
                act.sem_inc(bank_free[u], 1)

            def high(slot, n_use, dst, n):
                act.wait_ge(tp_done[slot], n_use + 1)
                nc.scalar.activation(dst, tp(slot, n), ACT.Copy).then_inc(hi_done[slot], 1)

            def x_high(n):
                for t in range(BT * n, BT * (n + 1)):
                    high(t % 2, t // 2, flat(xT_a[:, t, 0, :, :]), KB)

            def split_high(place, src, m):
                nc.scalar.activation(wa[:, place, 0, :], src, ACT.Copy, scale=mul[:, m:m + 1]).then_inc(split_hi, 1)

            x_high(0)
            x_high(1)
            x_high(2)
            act.wait_ge(scales_ready, 1)
            for j in range(4):
                act.wait_ge(max_full[j], 32)
                split_high(j, raw(j, KB * CW), AG)
                if j == 0:
                    x_high(3)

            def count(b, pair, k, j, both=False):
                if both and k:
                    act.wait_ge(act_count[0], pair_base(b, pair, NBITS, SLOTS) + j + 1)
                elif both and j:
                    act.wait_ge(act_count[1], b * sum(UP_B_STEPS) + j)
                act.wait_ge(cand_ready[k], pair_base(b, pair, NBITS + 1, SLOTS + 1) + j + 1)
                nc.scalar.activation(JUNK[:, 1, :], a_row[k], ACT.Sign, scale=-1.0,
                                     bias=cand[:, k:k + 1].bitcast(FP32), accum_out=cnt[:, k:k + 1])\
                    .then_inc(act_count[k], 1)

            for ph in range(4):
                m = AG if ph < 2 else AU
                if ph == 2:
                    act.wait_ge(scales_ready, 3)
                with act.Fori(0, 4) as i:
                    for tq in range(4):
                        g = i * 4 + (16 * ph + tq)
                        act.wait_ge(stored[tq % 2], i * 32 + (16 * (8 * ph + tq // 2 + 1)))
                        for u in range(BT):
                            act.wait_ge(mm_done[u], g + 1)
                            nc.scalar.activation(stage[tq % 2][:, u, :], PS[:, 4 + u, 0:CW],
                                                 ACT.Silu if ph < 2 else ACT.Copy, scale=un[:, m:m + 1])\
                                .then_inc(bank_free[u], 1)
                        if ph >= 2:
                            for k in range(2):
                                count(None, ph - 2, 0, i * 8 + (2 * tq + k))
                        if tq and (ph < 2 or tq == 1):
                            if ph < 2:
                                n, (_, _, _, _, cols, mi) = i * 3 + (12 * ph + tq - 1), UNITS[tq - 1]
                                width = KB * CW if mi != BD else IB * UW
                                src = raw(3, width)
                                act.wait_ge(w_ready, n + 1)
                            else:
                                n, width, mi, src = i + (24 + 4 * (ph - 2)), IB * UW, AD, raw(1, IB * UW)
                                act.wait_ge(unit_full, n * 16 + 16)
                            act.wait_ge(u_stored, n * 16 + 16)
                            nc.scalar.activation(raw(2, width).bitcast(FP16)[:, 0:width], src, ACT.Copy,
                                                 scale=mul[:, mi:mi + 1]).then_inc(u_hi, 1)
                    if ph < 3:
                        if ph == 1:
                            act.wait_ge(scales_ready, 2)
                        act.wait_ge(chunk_full, i * 16 + (64 * ph + 16))
                        alone(act)
                        split_high(i, raw(0, KB * CW), AG if ph == 0 else AU)

            def blocks(b, search):
                def h_high(g0, t):
                    for part, n in enumerate(TPARTS):
                        g = g0 + 3 * t + part
                        high(g % 2, use(b, g), flat(hT[:, t, 0, 8 * part:8 * part + n, :]), n)

                def x_high_b(t):
                    high(t % 2, use(b, T_X + t), flat(xT_b[:, t, 0, :, :]), KB)

                def y_rows(g0, layer, c, t):
                    if layer == 0 and c == 0 and t == 0:
                        act.wait_ge(out_stored, b * (16 * BT) + 16)
                    act.wait_ge(mm_done[t], group(b, g0 + c) + 1)
                    nc.scalar.activation(Y[:, t, 2 * UW * c:2 * UW * (c + 1)], PS[:, 4 + t, 0:2 * UW], ACT.Copy,
                                         scale=inv[:, layer, t:t + 1]).then_inc(bank_free[t], 1)

                def silu(c, t):
                    act.wait_ge(mm_done[t], group(b, G_GATE + c) + 1)
                    nc.scalar.activation(S[:, t, c * CW:(c + 1) * CW], PS[:, 4 + t, 0:CW], ACT.Silu,
                                         scale=un[:, BG:BG + 1]).then_inc(bank_free[t], 1)

                def first_group(transposed, product):
                    transposed(0)
                    transposed(1)
                    for t in range(BT):
                        product(0, t)
                        if t + 2 < BT:
                            transposed(t + 2)

                def counts(pair, j0, n, both=False):
                    for j in range(j0, j0 + n):
                        for k in range(2 if both else 1):
                            if search:
                                count(b, pair, k, j, both)

                j = 0
                for c in range(4):
                    if c == 0:
                        first_group(lambda t: h_high(0, t), lambda c, t: y_rows(0, 0, c, t))
                    else:
                        for t in range(BT):
                            y_rows(0, 0, c, t)
                    counts(0, j, DOWN_A_STEPS[c])
                    j += DOWN_A_STEPS[c]
                for c in range(NCH):
                    if c == 0:
                        first_group(x_high_b, silu)
                    else:
                        for t in range(BT):
                            silu(c, t)
                    counts(0, j, GATE_STEPS[c])
                    j += GATE_STEPS[c]
                j = 0
                for c in range(NCH):
                    counts(1, j, UP_B_STEPS[c], both=True)
                    j += UP_B_STEPS[c]
                act.wait_ge(x1_stored, b * (16 * BT) + 16 * (BT + 1))
                for c in range(4):
                    if c == 0:
                        first_group(lambda t: h_high(T_H, t), lambda c, t: y_rows(G_DOWN, 1, c, t))
                    else:
                        for t in range(BT):
                            y_rows(G_DOWN, 1, c, t)
                    counts(1, j, DOWN_B_STEPS[c])
                    j += DOWN_B_STEPS[c]

            for_blocks(act, blocks)

        @block.vector
        def _(dve):
            step = Steps(dve_steps)

            def then(ins, apart=False):
                dve.wait_ge(dve_steps, step.add(ins))
                if apart:
                    alone(dve)

            dve.sem_inc(u_lo, 1)
            dve.sem_inc(lo_done[0], 1)
            dve.sem_inc(lo_done[1], 1)
            dve.sem_inc(out_ready, 1)
            for j in range(SLOTS):
                nc.vector.memset(bitf[:, j:j + 1], float(2 ** (NBITS - 1 - j)) if j < NBITS else 0.0)
                nc.vector.memset(bitn[:, j:j + 1], 2 ** (NBITS - 2 - j) if j < NBITS - 1 else 0)
            nc.vector.memset(hmax[:, :, :], TINY)
            then(nc.vector.memset(mx[:, :], 0.0))

            dve.wait_ge(zs_full, 96)
            for n, (_, _, rows, cols) in enumerate(BOUNDS):
                z, s = (a[0:rows, 0:cols] for a in bounds_in[n])
                then(nc.vector.tensor_scalar(z.bitcast(INT32), z.bitcast(INT32), ABS_BITS, None, ALU.bitwise_and))
                then(nc.vector.scalar_tensor_tensor(out=z, in0=z, scalar=15.0, in1=s, op0=ALU.add, op1=ALU.mult))
                at = 24 + (BG, BU, BD)[n]
                then(nc.vector.tensor_reduce(out=mx[0:rows, at:at + 1], in_=z, op=ALU.max, axis=AX.X,
                                             apply_absolute_value=True))

            def maximum(at, src):
                nc.vector.tensor_reduce(out=mx[:, at], in_=src, op=ALU.max, axis=AX.X,
                                        apply_absolute_value=True).then_inc(max_read, 1)

            def scales(n, first, matrix, cols, x_cols):
                dve.wait_ge(max_read, first + 8)
                nc.vector.tensor_reduce(out=mx[:, 24 + matrix:25 + matrix], in_=mx[:, first:first + 8], op=ALU.max,
                                        axis=AX.X).then_inc(maxima_ready, 1)
                dve.wait_ge(global_ready, n)
                g = gmx[:, cols]
                then(nc.vector.tensor_scalar(g, g, TINY, None, ALU.max))
                then(nc.vector.tensor_scalar(g.bitcast(INT32), g.bitcast(INT32), EXP_BITS, None, ALU.bitwise_and))
                then(nc.vector.reciprocal(mul[:, cols], g))
                then(nc.vector.tensor_scalar(un[:, cols], g, 1.0 / TOP, None, ALU.mult))
                if x_cols:
                    then(nc.vector.tensor_scalar(un[:, x_cols], un[:, x_cols], 1.0 / XS, None, ALU.mult))
                nc.vector.tensor_scalar(mul[:, cols], mul[:, cols], TOP, None, ALU.mult).then_inc(scales_ready, 1)
                dve.wait_ge(scales_ready, n)

            def statistics(rows, t):
                h = D // 2
                nc.vector.bn_stats(st[:, t, 0:6], rows[:, 0:h])
                return nc.vector.bn_stats(st[:, t, 6:12], rows[:, h:D])

            def low(slot, n_use, dst, hi, n):
                dve.wait_ge(hi_done[slot], n_use + 1)
                nc.vector.tensor_tensor(dst, tp(slot, n), hi, ALU.subtract).then_inc(lo_done[slot], 1)

            def normalised(n):
                x = x_half[n % 2]
                dve.wait_ge(x_full[n], 16)
                for t in range(BT):
                    last = statistics(x[:, t, :], t)
                then(last)
                for t in range(BT):
                    last = nc.vector.bn_aggr(mv[:, t, :], st[:, t, :])
                then(last)
                nc.vector.tensor_scalar(mv[:, :, 1], mv[:, :, 1], EPS, None, ALU.add).then_inc(var_ready, 1)
                dve.wait_ge(rstd_ready, n + 1)
                then(nc.vector.tensor_scalar(rx[:, :], rs[:, :], XS, None, ALU.mult))
                for t in range(BT):
                    nc.vector.tensor_scalar(x[:, t, :], x[:, t, :], mv[:, t, 0:1], rx[:, t:t + 1], ALU.subtract,
                                            ALU.mult).then_inc(xs_ready, 1)

            def x_low(n):
                for t in range(BT * n, BT * (n + 1)):
                    low(t % 2, t // 2, flat(xT_a[:, t, 1, :, :]), flat(xT_a[:, t, 0, :, :]), KB)

            def split_low(n, place, src, m):
                dve.wait_ge(split_hi, n + 1)
                nc.vector.scalar_tensor_tensor(out=wa[:, place, 1, :], in0=src, scalar=mul[:, m:m + 1],
                                               in1=wa[:, place, 0, :], op0=ALU.mult, op1=ALU.subtract)\
                    .then_inc(split_lo, 1)

            normalised(0)
            for j in range(4):
                dve.wait_ge(max_full[j], 16)
                maximum(slice(j, j + 1), raw(j, KB * CW))
            normalised(1)
            x_low(0)
            for j in range(4):
                dve.wait_ge(max_full[j], 32)
                maximum(slice(4 + j, 5 + j), raw(j, KB * CW))
            scales(1, 0, AG, slice(0, 4), slice(0, 3))
            normalised(2)
            x_low(1)
            normalised(3)
            x_low(2)
            split_low(0, 0, raw(0, KB * CW), AG)
            x_low(3)
            for j in range(1, 4):
                split_low(j, j, raw(j, KB * CW), AG)
            dve.wait_ge(split_lo, 4)

            def dequantise(n, k, width, blocks):
                q = raw(1, blocks * width).bitcast(INT32).rearrange("p (j n) -> p j n", j=blocks)
                w = raw(3, 2 * blocks * width)
                w4 = w.rearrange("p (j e n) -> p j e n", j=blocks, e=2)
                wi = w.bitcast(INT32).rearrange("p (j e n) -> p j e n", j=blocks, e=2)
                dve.wait_ge(unit_full, n * 16 + 16)
                nc.vector.tensor_scalar(wi[:, :, 0, :], q, 4, 15, ALU.logical_shift_right, ALU.bitwise_and)
                then(nc.vector.tensor_scalar(wi[:, :, 1, :], q, 15, None, ALU.bitwise_and))
                dve.wait_ge(unit_zs, n * 32 + 32)
                if k < 2:
                    z, s = (a_row[d][:, 0:width].unsqueeze(1).to_broadcast([P, 2 * blocks, width]) for d in range(2))
                    w4, wi = (a.rearrange("p j e n -> p (j e) n") for a in (w4, wi))
                else:
                    z, s = (a_row[d][:, 0:blocks * width].rearrange("p (j n) -> p j n", j=blocks).unsqueeze(2)
                            .to_broadcast([P, blocks, 2, width]) for d in range(2))
                then(nc.vector.tensor_tensor(w4, wi, z, ALU.subtract))
                nc.vector.tensor_tensor(w4, w4, s, ALU.mult).then_inc(w_ready, 1)
                return w

            def unit_low(n, w, mi):
                width = w.shape[-1]
                hl = raw(2, width).bitcast(FP16)
                dve.wait_ge(u_hi, n + 1)
                nc.vector.scalar_tensor_tensor(out=hl[:, width:2 * width], in0=w, scalar=mul[:, mi:mi + 1],
                                               in1=hl[:, 0:width], op0=ALU.mult, op1=ALU.subtract).then_inc(u_lo, 1)

            for ph in range(2):
                with dve.Fori(0, 4) as i:
                    kept = step.enter(i, 6)
                    for k, (_, _, _, _, _, mi) in enumerate(UNITS):
                        n = i * 3 + (12 * ph + k)
                        dve.wait_ge(u_lo, n + 1)
                        unit_low(n, dequantise(n, k, CW if k < 2 else UW, KB // 2 if k < 2 else JB), mi)
                        if k != 1:
                            dve.wait_ge(max_next, i * 32 + (128 * ph + 16 * (k // 2 + 1)))
                            alone(dve)
                            maximum(bass.ds(i * 2 + (8 * (ph + 1) + k // 2), 1),
                                    m_row[:, 0:KB * CW if ph == 0 else IB * UW])
                    split_low(i + 4 * (ph + 1), i, raw(0, KB * CW), AG if ph == 0 else AU)
                    step.leave(kept, 4)
                scales(2 + ph, 8 * (ph + 1), AU + ph, slice(4 + ph, 5 + ph), slice(4, 5) if ph == 0 else None)

            def start_pair(b, pair, n_full):
                for k in range(2):
                    dve.wait_ge(s_full[k], n_full)
                    a = a_row[k].bitcast(INT32)
                    nc.vector.tensor_scalar(a, a, ABS_BITS, None, ALU.bitwise_and)
                for k in range(2):
                    nc.vector.memset(cand[:, k:k + 1], 2 ** (NBITS - 1)).then_inc(cand_ready[k], 1)

            def search_step(b, pair, j, j_expr=None, act_counts_both=False):
                at = j if j_expr is None else j_expr
                base = pair_base(b, pair, NBITS + 1, SLOTS + 1)
                if j_expr is None:
                    bit, nxt = bitf[:, j:j + 1], bitn[:, j:j + 1]
                else:
                    bit, nxt = bitf[:, bass.ds(j_expr, 1)], bitn[:, bass.ds(j_expr, 1)]

                def decide(k, on_act):
                    f = flip[:, k:k + 1]
                    then(nc.vector.tensor_scalar(f, cnt[:, k:k + 1], 0.0 if on_act else DROPPED - 0.5, bit,
                                                 ALU.is_ge, ALU.mult))
                    nc.vector.scalar_tensor_tensor(out=cand[:, k:k + 1], in0=cand[:, k:k + 1], scalar=f, in1=nxt,
                                                   op0=ALU.bitwise_xor, op1=ALU.bitwise_xor)\
                        .then_inc(cand_ready[k], 1)

                if not act_counts_both:
                    dve.wait_ge(cand_ready[1], base + at + 1)
                    counted = nc.vector.tensor_scalar(JUNK[:, 0, :], a_row[1], cand[:, 1:2].bitcast(FP32), None,
                                                      ALU.is_lt, ALU.add, accum_out=cnt[:, 1:2])
                    value = step.add(counted)
                dve.wait_ge(act_count[0], pair_base(b, pair, NBITS, SLOTS) + at + 1)
                decide(0, True)
                if act_counts_both:
                    dve.wait_ge(act_count[1], b * sum(UP_B_STEPS) + (at + 1))
                else:
                    dve.wait_ge(dve_steps, value)
                decide(1, act_counts_both)

            def threshold(b, pair, k):
                T = cand[:, k:k + 1]
                a = a_row[k]
                dve.wait_ge(cand_ready[k], (pair_base(b, pair, NBITS + 1, SLOTS + 1) + NBITS + 1) if b is not None
                            else (SLOTS + 1) * (pair + 1))
                then(nc.vector.tensor_scalar(JUNK[:, 0, :], a, T.bitcast(FP32), None, ALU.is_le, ALU.add,
                                             accum_out=cnt[:, k:k + 1]))
                nc.vector.tensor_scalar(fin[:, k:k + 1], cnt[:, k:k + 1], DROPPED - 0.5, None, ALU.is_ge)
                then(nc.vector.tensor_scalar(flip[:, k:k + 1], cnt[:, k:k + 1], DROPPED - 0.5, None, ALU.is_le),
                     apart=True)
                then(nc.vector.tensor_tensor(T, T, flip[:, k:k + 1], ALU.add))
                then(nc.vector.tensor_scalar(JUNK[:, 0, :], a, T.bitcast(FP32), None, ALU.is_equal))

            def ties(k, n_kill):
                then(nc.vector.tensor_tensor_scan(a_row[2], JUNK[:, 0, :], JUNK[:, 0, :], 0.0, ALU.add, ALU.bypass))
                then(nc.vector.tensor_tensor(fin[:, k:k + 1], fin[:, k:k + 1], a_row[2][:, I - 1:I], ALU.mult))
                then(nc.vector.tensor_tensor(fin[:, k:k + 1], fin[:, k:k + 1], cnt[:, k:k + 1], ALU.subtract))
                then(nc.vector.tensor_scalar(fin[:, k:k + 1], fin[:, k:k + 1], float(DROPPED), None, ALU.add))
                nc.vector.scalar_tensor_tensor(out=JUNK[:, 0, :], in0=a_row[2], scalar=fin[:, k:k + 1],
                                               in1=JUNK[:, 0, :], op0=ALU.is_le, op1=ALU.mult).then_inc(kill_ready, 1)
                dve.wait_ge(kill_ready, n_kill)

            def masked(k, n_again):
                a = a_row[k]
                then(nc.vector.scalar_tensor_tensor(out=a, in0=a, scalar=cand[:, k:k + 1].bitcast(FP32),
                                                    in1=JUNK[:, 0, :], op0=ALU.is_ge, op1=ALU.subtract))
                dve.wait_ge(s_again, 16 * n_again if isinstance(n_again, int) else n_again * 16)
                nc.vector.tensor_tensor(a, a, a_row[2], ALU.mult).then_inc(m_ready, 1)

            def mask(b, pair, k):
                first = 2 * pair if b is None else b * BT + (BT + 2 * pair)
                if k:
                    dve.wait_ge(m_ready, first + k)
                threshold(b, pair, k)
                ties(k, first + (k + 1))
                masked(k, first + (k + 1))

            def scales_of(tiles, maxima):
                a = hs[:, 0, tiles]
                then(nc.vector.tensor_reduce(out=a, in_=maxima, op=ALU.max, axis=AX.X))
                then(nc.vector.reciprocal(a, a))
                then(nc.vector.tensor_scalar(a.bitcast(INT32), a.bitcast(INT32), EXP_BITS, None, ALU.bitwise_and))

            def scaled(t, ready):
                rows = S[:, t, 0:I]
                nc.vector.tensor_scalar(rows, rows, hs[:, 0, t:t + 1], H_TOP, ALU.mult, ALU.mult).then_inc(ready, 1)

            def unscales_of(tiles, layer, matrix):
                then(nc.vector.reciprocal(hs[:, 1, tiles], hs[:, 0, tiles]))
                then(nc.vector.tensor_scalar(inv[:, layer, tiles], hs[:, 1, tiles], 1.0 / H_TOP,
                                             un[:, matrix:matrix + 1], ALU.mult, ALU.mult))

            def layer_a_h(t, n_row, tile):
                rows = S[:, t, 0:I]
                dve.wait_ge(row_full[t], n_row)
                dve.wait_ge(u_full, 16 * (tile + 1) if isinstance(tile, int) else tile * 16 + 16)
                nc.vector.tensor_tensor(rows, rows, a_row[2], ALU.mult).then_inc(u_read, 1)
                dve.wait_ge(u_read, tile + 1)
                then(nc.vector.tensor_reduce(out=hmax[:, t, 0:1], in_=rows, op=ALU.max, axis=AX.X,
                                             apply_absolute_value=True))
                scales_of(slice(t, t + 1), hmax[:, t, 0:NCH + 1:NCH])
                scaled(t, h_ready)
                unscales_of(slice(t, t + 1), 0, AD)

            for ph in range(2, 4):
                start_pair(None, ph - 2, 16 * (ph - 1))
                with dve.Fori(0, 4) as i:
                    n = i + (24 + 4 * (ph - 2))
                    kept = step.enter(i, 3 * 8)
                    for tq in range(4):
                        for k in range(2):
                            search_step(None, ph - 2, None, i * 8 + (2 * tq + k))
                        if tq == 1:
                            unit_low(n, raw(1, IB * UW), AD)
                    if ph == 2:
                        split_low(i + 12, i, raw(0, KB * CW), AU)
                    step.leave(kept, 4)
                for k in range(2):
                    mask(None, ph - 2, k)
            for t in range(BT):
                layer_a_h(t, 16, t)

            def blocks(b, search):
                def h_low(g0, t):
                    for part, n in enumerate(TPARTS):
                        g = g0 + 3 * t + part
                        low(g % 2, use(b, g), flat(hT[:, t, 1, 8 * part:8 * part + n, :]),
                            flat(hT[:, t, 0, 8 * part:8 * part + n, :]), n)

                def x_low_b(t):
                    low(t % 2, use(b, T_X + t), flat(xT_b[:, t, 1, :, :]), flat(xT_b[:, t, 0, :, :]), KB)

                def mean_rstd(t, n):
                    then(statistics(Y[:, t, :], t), apart=True)
                    then(nc.vector.bn_aggr(mv[:, t, :], st[:, t, :]))
                    nc.vector.tensor_scalar(mv[:, t, 1:2], mv[:, t, 1:2], EPS, None, ALU.add).then_inc(var_ready, 1)
                    dve.wait_ge(rstd_ready, b * (3 * BT) + (4 + n + 1))

                def normalise(t):
                    y = Y[:, t, :]
                    then(nc.vector.tensor_scalar(y, y, mv[:, t, 0:1], rs[:, t:t + 1], ALU.subtract, ALU.mult))

                def x1(t):
                    y = Y[:, t, :]
                    dve.wait_ge(bank_free[t], group(b, 3) + 2)
                    mean_rstd(t, 2 * t)
                    normalise(t)
                    dve.wait_ge(row_full[t], b * 32 + 32)
                    nc.vector.tensor_tensor(y, y, S[:, t, 0:D], ALU.add).then_inc(x1_ready, 1)
                    dve.wait_ge(x1_ready, b * BT + (t + 1))
                    mean_rstd(t, 2 * t + 1)
                    then(nc.vector.tensor_scalar(rx[:, t:t + 1], rs[:, t:t + 1], XS, None, ALU.mult))
                    nc.vector.tensor_scalar(S[:, t, D:2 * D], y, mv[:, t, 0:1], rx[:, t:t + 1], ALU.subtract,
                                            ALU.mult).then_inc(xs_ready, 1)

                def out_rows(t):
                    y = Y[:, t, :]
                    dve.wait_ge(bank_free[t], group(b, G_PER - 1) + 2)
                    mean_rstd(t, 2 * BT + t)
                    normalise(t)
                    dve.wait_ge(x1_full, b * (16 * BT) + 16 * (t + 1))
                    nc.vector.tensor_tensor(y, y, x1_row, ALU.add).then_inc(out_ready, 1)

                def steps(pair, j0, n, both=False):
                    for j in range(j0, j0 + n):
                        if search:
                            search_step(b, pair, j, act_counts_both=both)

                def times_s(c, t):
                    dve.wait_ge(mm_done[t], group(b, G_UP + c) + 1)
                    rows = S[:, t, c * CW:(c + 1) * CW]
                    nc.vector.scalar_tensor_tensor(out=rows, in0=PS[:, 4 + t, 0:CW], scalar=un[:, BU:BU + 1],
                                                   in1=rows, op0=ALU.mult, op1=ALU.mult).then_inc(bank_free[t], 1)

                def maximum_of(c, t):
                    dve.wait_ge(bank_free[t], group(b, G_UP + c) + 2)
                    return nc.vector.tensor_reduce(out=hmax[:, t, c:c + 1], in_=S[:, t, c * CW:(c + 1) * CW],
                                                   op=ALU.max, axis=AX.X, apply_absolute_value=True)

                per = BT * 6 + 6 + BT * 3
                if search:
                    per += 3 * (NBITS + NBITS - sum(UP_B_STEPS)) + 2 * sum(UP_B_STEPS) + 4 * 9 + BT * 6
                kept = step.enter(b, per) if search else None
                j = 0
                for c in range(4):
                    if c == 0:
                        for t in range(BT):
                            h_low(0, t)
                        if search:
                            start_pair(b, 0, b * 32 + 48)
                    steps(0, j, DOWN_A_STEPS[c])
                    j += DOWN_A_STEPS[c]
                for t in range(BT):
                    x1(t)
                for c in range(NCH):
                    if c == 0:
                        for t in range(BT):
                            x_low_b(t)
                    steps(0, j, GATE_STEPS[c])
                    j += GATE_STEPS[c]
                if search:
                    mask(b, 0, 0)
                    mask(b, 0, 1)
                    start_pair(b, 1, b * 32 + 64)
                j = 0
                for c in range(NCH):
                    for t in range(BT):
                        times_s(c, t)
                        if t:
                            maximum_of(c, t - 1)
                        if t >= BT - UP_B_STEPS[c]:
                            steps(1, j, 1, both=True)
                            j += 1
                    last = maximum_of(c, BT - 1)
                then(last)
                scales_of(slice(0, BT), hmax[:, :, :])
                for t in range(BT):
                    scaled(t, hb_ready)
                    if t == 1:
                        unscales_of(slice(0, BT), 1, BD)
                    if t:
                        h_low(T_H, t - 1)
                h_low(T_H, BT - 1)
                first = b * BT + BT
                for c in range(4):
                    if search and c == 0:
                        layer_a_h(0, b * 32 + 48, first)
                        layer_a_h(1, b * 32 + 48, first + 1)
                    n = DOWN_B_STEPS[c]
                    steps(1, j, n)
                    j += n
                if search:
                    mask(b, 1, 0)
                    mask(b, 1, 1)
                    layer_a_h(2, b * 32 + 48, first + 2)
                    layer_a_h(3, b * 32 + 48, first + 3)
                for t in range(BT):
                    out_rows(t)
                if search:
                    step.leave(kept, NB - 1)

            for_blocks(dve, blocks)

        @block.tensor
        def _(pe):
            def transposes(slot, n_use, source, n):
                pe.wait_ge(lo_done[slot], n_use + 1)
                for k in range(n):
                    rows = source(k)
                    m = rows.shape[-1]
                    last = nc.tensor.transpose(tp(slot, n)[0:m, k * P:(k + 1) * P], rows, ident[:, :])
                last.then_inc(tp_done[slot], 1)

            def products(bank, lhs, rhs, blocks, width, rows_last=P):
                n = 0
                for kb in range(blocks):
                    m = rows_last if kb >= blocks - 2 else P
                    for hx, hw in ((0, 0), (0, 1), (1, 0)):
                        last = nc.tensor.matmul(PS[:, 4 + bank, 0:width], lhs(hx, kb, m), rhs(hw, kb, m),
                                                start=n == 0, stop=n == 3 * blocks - 1)
                        n += 1
                last.then_inc(mm_done[bank], 1)

            pe.wait_ge(ident_ready, 1)
            with pe.Fori(0, NT // (2 * BT)) as i:
                for u in range(2 * BT):
                    rows = x_half[u // BT][:, u % BT, :].rearrange("p (a k) -> p k a", k=KB)
                    pe.wait_ge(xs_ready, i * (2 * BT) + (u + 1))
                    transposes(u % 2, i * BT + u // 2, lambda k: rows[:, k, :], KB)
            for s in range(2):
                pe.wait_ge(lo_done[s], NT // 2 + 1)
            with pe.Fori(0, 4) as ph:
                with pe.Fori(0, 4) as i:
                    pe.wait_ge(split_lo, ph * 4 + i + 1)
                    alone(pe)
                    with pe.Fori(0, NT // BT) as tq:
                        for u in range(BT):
                            pe.wait_ge(bank_free[u], ph * 16 + i * 4 + tq + 1)
                            products(u, lambda h, kb, m: xT_a[:, tq * BT + u, h, kb, :],
                                     lambda h, kb, m: wa[:, i, h, kb * CW:(kb + 1) * CW], KB, CW)

            def blocks(b, search):
                def split(g):
                    pe.wait_ge(lo_done[g % 2], use(b, g) + 2)

                def h_transposed(g0, ready, n_ready, t):
                    pe.wait_ge(ready, n_ready + (t + 1))
                    alone(pe)
                    rows = S[:, t, :].rearrange("p (j m e) -> p j e m", j=JB, e=2)
                    for part, n in enumerate(TPARTS):
                        g = g0 + 3 * t + part

                        def block_rows(k):
                            kb = 8 * part + k
                            return rows[:, kb // 2, kb % 2, 0:PL if kb >= IB - 2 else P]

                        transposes(g % 2, use(b, g), block_rows, n)

                def down(g0, n0, c, t):
                    n = n0 + c
                    if t == 0:
                        pe.wait_ge(w_full[n % 2], b * 128 + 16 * (n // 2 + 1))
                        alone(pe)
                    pe.wait_ge(bank_free[t], group(b, g0 + c) + 1)
                    products(t, lambda h, kb, m: hT[0:m, t, h, kb, :],
                             lambda h, kb, m: w_down[n % 2][0:m, :, h, kb, :], IB, 2 * UW, PL)

                def gate_up(g0, n0, c, t):
                    n = n0 + c // 2
                    if t == 0 and c % 2 == 0:
                        pe.wait_ge(w_full[n % 2], b * 128 + 16 * (n // 2 + 1))
                        alone(pe)
                    pe.wait_ge(bank_free[t], group(b, g0 + c) + 1)
                    products(t, lambda h, kb, m: xT_b[:, t, h, kb, :],
                             lambda h, kb, m: w_gu(n % 2, c % 2)[:, h, kb, :], KB, CW)

                def first_group(transposed, groups, product):
                    transposed(0)
                    transposed(1)
                    for t in range(BT):
                        for g in groups(t)[-2:]:
                            split(g)
                        product(0, t)
                        if t + 2 < BT:
                            transposed(t + 2)

                def h_groups(g0):
                    return lambda t: [g0 + 3 * t + part for part in range(3)]

                def x_transposed(t):
                    pe.wait_ge(xs_ready, b * BT + (NT + t + 1))
                    alone(pe)
                    rows = S[:, t, D:2 * D].rearrange("p (a k) -> p k a", k=KB)
                    transposes(t % 2, use(b, T_X + t), lambda k: rows[:, k, :], KB)

                first_group(lambda t: h_transposed(0, h_ready, b * BT, t), h_groups(0),
                            lambda c, t: down(0, 0, c, t))
                for c in range(1, 4):
                    for t in range(BT):
                        down(0, 0, c, t)
                first_group(x_transposed, lambda t: [T_X + t], lambda c, t: gate_up(G_GATE, 4, c, t))
                for c in range(1, 2 * NCH):
                    for t in range(BT):
                        gate_up(G_GATE, 4, c, t)
                first_group(lambda t: h_transposed(T_H, hb_ready, b * BT, t), h_groups(T_H),
                            lambda c, t: down(G_DOWN, 12, c, t))
                for c in range(1, 4):
                    for t in range(BT):
                        down(G_DOWN, 12, c, t)

            for_blocks(pe, blocks)


_NAMES = ["x", "wg_a", "wu_a", "wd_a", "qg", "qu", "qd", "sg", "zg", "su", "zu", "sd", "zd"]


def kernel(L0_attn_x, L0_attn_w_gate, L0_attn_w_up, L0_attn_w_down, L0_ffn_gate_Wq, L0_ffn_up_Wq, L0_ffn_down_Wq,
           L0_ffn_gate_scale, L0_ffn_gate_zero, L0_ffn_up_scale, L0_ffn_up_zero, L0_ffn_down_scale, L0_ffn_down_zero):
    import numpy as np
    import concourse.bacc as bacc
    from concourse.bass_utils import run_bass_kernel_spmd

    def contraction_chunks(w):
        w = np.asarray(w).T
        return w.reshape(P, w.shape[0] // P, NCH, CW).transpose(2, 0, 1, 3)

    def group_chunks(a):
        a = np.asarray(a).T
        return a.reshape(a.shape[0], NCH, CW).transpose(1, 0, 2)

    def padded(w, rows):
        w = np.asarray(w).T
        return np.concatenate([w, np.zeros((rows - w.shape[0], w.shape[1]), w.dtype)])

    def down_units(w):
        w = padded(w, IB * P).reshape(JB, P, 2, NU, UW)
        return w.transpose(3, 1, 0, 2, 4).reshape(NU, P, IB * UW)

    def packed_units(w):
        w = padded(w, JB * P).reshape(JB, P, NU, UW)
        return w.transpose(2, 1, 0, 3).reshape(NU, P, JB * UW)

    def group_units(a):
        a = padded(a, JB * 4).reshape(JB, 4, NU, UW)
        return a.transpose(2, 1, 0, 3).reshape(NU, 4, JB * UW)

    arrays = {
        "x": np.asarray(L0_attn_x).reshape(NT, P, D),
        "wg_a": contraction_chunks(L0_attn_w_gate).reshape(NCH, P, KB * CW),
        "wu_a": contraction_chunks(L0_attn_w_up).reshape(NCH, P, KB * CW),
        "wd_a": down_units(L0_attn_w_down),
        "qg": contraction_chunks(L0_ffn_gate_Wq).reshape(NCH, P, KB // 2 * CW),
        "qu": contraction_chunks(L0_ffn_up_Wq).reshape(NCH, P, KB // 2 * CW),
        "qd": packed_units(L0_ffn_down_Wq),
        "sg": group_chunks(L0_ffn_gate_scale), "zg": group_chunks(L0_ffn_gate_zero),
        "su": group_chunks(L0_ffn_up_scale), "zu": group_chunks(L0_ffn_up_zero),
        "sd": group_units(L0_ffn_down_scale), "zd": group_units(L0_ffn_down_zero),
    }
    arrays = {n: np.ascontiguousarray(a) for n, a in arrays.items()}
    nc = bacc.Bacc("TRN2", target_bir_lowering=False, num_devices=1)
    args = [nc.dram_tensor(f"in_{n}", arrays[n].shape, mybir.dt.from_np(arrays[n].dtype), kind="ExternalInput").ap()
            for n in _NAMES]
    out = nc.dram_tensor("out", (NT, P, D), FP32, kind="ExternalOutput").ap()
    build(nc, *args, out)
    r = run_bass_kernel_spmd(nc, [{f"in_{n}": arrays[n] for n in _NAMES}], core_ids=[0])
    return r.results[0]["out"].reshape(1, TOKENS, D)
```

```python
from contextlib import ExitStack

import concourse.bass as bass
from concourse import mybir

FP32 = mybir.dt.float32
FP16 = mybir.dt.float16
INT32 = mybir.dt.int32
INT16 = mybir.dt.int16
BF16 = mybir.dt.bfloat16
U8 = mybir.dt.uint8
ALU = mybir.AluOpType
ACT = mybir.ActivationFunctionType
AX = mybir.AxisListType
RMAX = bass.bass_isa.ReduceOp.max

P = 128
TOKENS, D, I, GROUP = 2048, 1024, 2752, 64
NT = TOKENS // P
KB = D // P
NCH = 8
CW = I // NCH
JB = (I // 2 + P - 1) // P
IB = 2 * JB
PL = I // 2 - (JB - 1) * P
NU, UW = 8, D // 8
GU, DU = 2 * KB * CW, 2 * IB * UW
BT = 4
NB = NT // BT
DROPPED = I // 2
EPS = 1e-5
TOP = 2.0 ** 14
H_TOP = 2.0 ** 15
XS = 2.0 ** 10
TINY = 2.0 ** -100
EXP_BITS, ABS_BITS = 0x7F800000, 0x7FFFFFFF
NBITS = 31
AG, BG, BU, BD, AU, AD = range(6)
TPARTS = (8, 8, IB - 16)

UP_STEPS = (2, 3, 3, 3)
TOP_STEPS = NBITS - 16
SLOTS = 3 * sum(UP_STEPS)
DOWN_A_STEPS = ((0, 0, 1, 2), (2, 2, 2, 2), (2, 2, 2, 2), (0, 0, 0, 0))
GATE_STEPS = ((0, 0, 0, 1), (1, 1, 1, 1), (1, 1, 1, 1), (1, 1, 1, 0)) + ((0,) * 4,) * 4
UP_B_STEPS = ((1,) * 4,) * 7 + ((0,) * 4,)
DOWN_B_STEPS_AT = ((0, 3), (1, 0), (1, 1))
SUMS_AT = ((0, 3), (1, 0), (2, 1), (2, 3))


class Steps:

    def __init__(self, sem):
        self.sem, self.base, self.n = sem, 0, 0

    def add(self, instruction, by=1):
        instruction.then_inc(self.sem, by)
        self.n += by
        return self.base + self.n

    def enter(self, i, per):
        kept = (self.base, self.n, per)
        self.base, self.n = i * per + (self.base + self.n), 0
        return kept

    def leave(self, kept, rounds):
        base, n, per = kept
        assert self.n == per, (self.n, per)
        self.base, self.n = base, n + rounds * per


def build(nc, x_in, wg_a, wu_a, wd_a, qg, qu, qd, sg, zg, su, zu, sd, zd, out):
    ctx = ExitStack()
    with ctx:
        def sb(name, shape, dt):
            return ctx.enter_context(nc.sbuf_tensor(name, shape, dt))

        def sem(name):
            return ctx.enter_context(nc.semaphore(name))

        def sems(name, n):
            return [sem(f"{name}{j}") for j in range(n)]

        def dram(name, shape, dt):
            return nc.dram_tensor(name, shape, dt, kind="Internal").ap()

        s_dram = dram("s_dram", (NT, P, I), FP32)
        m_dram = dram("m_dram", (NT, P, I), FP32)
        u_dram = dram("u_dram", (NT, P, I), FP32)
        x1_dram = dram("x1_dram", (NT, P, D), FP32)
        first_dram = dram("first_dram", (6 + BT, P, 1), FP32)
        wd_dram = [dram(f"wd{n}_dram", (NU, P, DU), FP16) for n in range(2)]
        wgu_dram = [dram(f"wgu{n}_dram", (NCH, P, GU), FP16) for n in range(2)]

        TR = sb("transposed", [P, NT * 2 * KB * P], FP16)
        W = sb("weights", [P, 2, 2 * DU], FP16)
        S = sb("rows", [P, BT, IB * P], FP32)
        A = sb("search_rows", [P, 3 * I + 64], FP32)
        JUNK = sb("junk", [P, 2, IB * P], U8)
        Y = sb("y_rows", [P, BT, D], FP32)
        ident = sb("ident", [P, P], FP32)
        bitf = sb("bit_values", [P, SLOTS], FP32)
        bitn = sb("next_bits", [P, SLOTS], INT32)
        mx = sb("bounds", [P, 24 + 6], FP32)
        gmx = sb("global_bounds", [P, 6], FP32)
        mul = sb("scales", [P, 6], FP32)
        un = sb("unscales", [P, 6], FP32)
        st = sb("stats", [P, BT, 12], FP32)
        mv = sb("mean_var", [P, BT, 2], FP32)
        rs = sb("rstd", [P, BT], FP32)
        rx = sb("rstd_scaled", [P, BT], FP32)
        half = sb("minus_half", [P, BT], FP32)
        cand = sb("candidates", [P, 2], INT32)
        flip = sb("flips", [P, 2], INT32)
        cnt = sb("counts", [P, 2], FP32)
        fin = sb("ranks_dropped", [P, 4], FP32)
        hsum = sb("h_sums", [P, BT, NCH + 1], FP32)
        hs = sb("h_scales", [P, 2, BT], FP32)
        inv = sb("h_unscales", [P, 2, BT], FP32)
        PS = ctx.enter_context(nc.psum_tensor("psum", [P, 8, 512], FP32))

        xT_a = TR[:, :].rearrange("p (t h k m) -> p t h k m", t=NT, h=2, k=KB)
        HB, XB = BT * 2 * IB * P, BT * 2 * KB * P
        hT = TR[:, 0:HB].rearrange("p (t h k m) -> p t h k m", t=BT, h=2, k=IB)
        junk_b = TR[:, 0:NCH * BT * CW].rearrange("p (c t n) -> p c t n", c=NCH, t=BT)
        xT_b = TR[:, HB:HB + XB].rearrange("p (t h k m) -> p t h k m", t=BT, h=2, k=KB)
        x1_row = TR[:, HB + XB:HB + XB + 2 * D].bitcast(FP32)
        a_row = [A[:, k * I:(k + 1) * I] for k in range(3)]
        upper = a_row[2][:, 0:I // 2].bitcast(BF16)
        upper_junk = a_row[2][:, I // 2:I].bitcast(BF16)
        mag_row = A[:, 2 * I:2 * I + IB * UW]
        x_half = [A[:, n * BT * D:(n + 1) * BT * D].rearrange("p (t n) -> p t n", t=BT) for n in range(2)]
        x_place = [x_half[0], x_half[1], Y[:, :, :], x_half[0]]
        wa = W[:, :, :].rearrange("p s n -> p (s n)")[:, 0:4 * GU].rearrange("p (c h n) -> p c h n", c=4, h=2)
        w_down = [W[:, s, :].rearrange("p (u h k n) -> p u h k n", u=2, h=2, k=IB) for s in range(2)]
        w_f32 = W[:, :, :].rearrange("p s n -> p (s n)").bitcast(FP32)
        ZW = JB * UW
        bounds_in = [(w_f32[:, (2 * n) * ZW:(2 * n + 1) * ZW], w_f32[:, (2 * n + 1) * ZW:(2 * n + 2) * ZW])
                     for n in range(3)]

        def w_gu(slot, part):
            return W[:, slot, part * GU:(part + 1) * GU].rearrange("p (h k n) -> p h k n", h=2, k=KB)

        def tp(slot, n):
            return PS[:, 2 * slot:2 * slot + 2, :].rearrange("p b n -> p (b n)")[:, 0:n * P]

        def raw(slot, n):
            return S[:, slot, 0:n]

        def flat(ap):
            return ap.rearrange("p k m -> p (k m)")

        stage = [Y[:, 2 * g:2 * g + 2, :].rearrange("p a n -> p (a n)")[:, 0:BT * CW]
                 .rearrange("p (u n) -> p u n", u=BT) for g in range(2)]
        BOUNDS = ((zg, sg, P, CW), (zu, su, P, CW), (zd, sd, 4 * NU, ZW))
        UNITS = ((qg, zg, sg, KB, CW, BG), (qu, zu, su, KB, CW, BU), (qd, zd, sd, 32, ZW, BD))

        ident_ready = sem("ident_ready")
        zs_full, x_full = sem("zs_full"), sems("x_full", 4)
        mag_full = sems("mag_full", 4)
        mag_next = sem("mag_next")
        mag_read = sem("mag_read")
        bounds_ready, global_ready = sem("bounds_ready"), sem("global_ready")
        scales_ready = sem("scales_ready")
        var_ready, rstd_ready = sem("var_ready"), sem("rstd_ready")
        xs_ready = sem("xs_ready")
        tp_done = sems("tp_done", 2)
        hi_done = sems("hi_done", 2)
        lo_done = sems("lo_done", 2)
        chunk_full = sem("chunk_full")
        split_hi, split_lo = sem("split_hi"), sem("split_lo")
        unit_full, unit_zs = sem("unit_full"), sem("unit_zs")
        w_ready = sem("w_ready")
        u_hi, u_lo = sem("unit_hi"), sem("unit_lo")
        u_stored = sem("unit_stored")
        mm_done = sems("mm_done", BT)
        bank_free = sems("bank_free", BT)
        stored = sems("stored", 2)
        s_full = sems("s_full", 2)
        cand_ready = sems("cand_ready", 2)
        act_count = sem("act_count")
        kill_ready, s_again = sem("kill_ready"), sem("s_again")
        m_ready, m_stored = sem("masked_ready"), sems("masked_stored", 2)
        m_full = sem("masked_full")
        us_ready = sem("us_ready")
        su_ready, sum_ready = sem("su_ready"), sem("sum_ready")
        h_ready = sem("h_ready")
        row_full = sems("row_full", BT)
        x1_full = sem("x1_full")
        w_full = sems("w_full", 2)
        x1_ready, x1_stored = sem("x1_ready"), sem("x1_stored")
        hb_ready = sem("hb_ready")
        out_ready, out_stored = sem("out_ready"), sems("out_stored", BT)
        dve_steps, pool_steps = sem("dve_steps"), sem("pool_steps")
        passed = {e.engine: sem(f"passed{n}") for n, e in
                  enumerate((nc.sync, nc.scalar, nc.vector, nc.gpsimd, nc.tensor))}

        def alone(engine):
            engine.sem_inc(passed[engine.engine], 1)

        block = ctx.enter_context(nc.Block())

        G_BLOCKS, G_PER = 2 * NCH * NB, 4 + NCH + NCH + 4
        G_GATE, G_UP, G_DOWN = 4, 4 + NCH, 4 + 2 * NCH
        T_BLOCKS, T_PER = (NT + 6) // 2, (3 * BT + BT + 3 * BT) // 2
        T_X, T_H = 6, 6 + BT
        T_A = (T_H + 3 * BT, T_H + 3 * BT + 3, 0, 3)

        def group(b, g):
            return b * G_PER + (G_BLOCKS + g)

        def use(b, g):
            return b * T_PER + (T_BLOCKS + g // 2)

        def pair_base(b, pair, per, per_up):
            return per_up * pair if b is None else (b * 2 + pair) * per + 2 * per_up

        def rounds(engine, body):
            with engine.Fori(0, 3) as i:
                body(i, True)
            body(3, False)

        def for_blocks(engine, body):
            with engine.Fori(0, NB - 1) as b:
                body(b, True)
            body(NB - 1, False)

        @block.sync
        def _(sp):
            def x_batch(n):
                if n == 3:
                    for s in range(2):
                        sp.wait_ge(tp_done[s], 2)
                sp.dma_start(x_place[n], x_in[BT * n:BT * (n + 1)].rearrange("t p n -> p t n"))\
                    .then_inc(x_full[n], 16)

            def chunk_in(j):
                if j >= 4:
                    sp.wait_ge(mag_read, j - 3)
                sp.dma_start(raw(j % 4, KB * CW), wg_a[(j + 4) % 8]).then_inc(mag_full[j % 4], 16)

            x_batch(0)
            x_batch(1)
            chunk_in(0)
            chunk_in(1)
            x_batch(2)
            chunk_in(2)
            for n, (z, s, rows, cols) in enumerate(BOUNDS):
                for dst, src in zip(bounds_in[n], (z, s)):
                    sp.dma_start(dst[0:rows, 0:cols], src.rearrange("c g n -> (c g) n")).then_inc(zs_full, 16)
            chunk_in(3)
            x_batch(3)
            for j in range(4, 8):
                chunk_in(j)
            for s in range(2):
                sp.wait_ge(tp_done[s], NT // 2)
            sp.wait_ge(split_lo, 4)

            def chunk(i, ph):
                src, off = (wg_a, 4) if ph == 0 else (wu_a, 4 * (ph - 1))
                sp.wait_ge(split_lo, i + 4 * (ph + 1))
                alone(sp)
                sp.dma_start(raw(0, KB * CW), src[i + off]).then_inc(chunk_full, 16)

            def unit(n, src, c, width, zeros_scales=None):
                sp.wait_ge(w_ready if zeros_scales else u_lo, n + 1)
                alone(sp)
                dst = raw(1, width).bitcast(INT32) if zeros_scales else raw(1, width)
                sp.dma_start(dst, src[c]).then_inc(unit_full, 16)
                if zeros_scales:
                    z, s, rep, cols = zeros_scales
                    for k, a in ((0, z), (1, s)):
                        sp.dma_start(a_row[k][:, 0:cols], a[c].unsqueeze(1).to_broadcast([P // rep, rep, cols]))\
                            .then_inc(unit_zs, 16)

            def for_magnitudes(i, ph, k):
                src, n = (wu_a, KB * CW) if ph == 0 else (wd_a, IB * UW)
                sp.wait_ge(mag_read, i * 2 + (8 * (ph + 1) + k))
                alone(sp)
                sp.dma_start(mag_row[:, 0:n], src[i * 2 + k]).then_inc(mag_next, 16)

            for ph in range(2):
                with sp.Fori(0, 4) as i:
                    chunk(i, ph)
                    for k, (q, z, s, rep, cols, _) in enumerate(UNITS):
                        unit(i * 3 + (12 * ph + k), q, i + 4 * ph, q.shape[-1], (z, s, rep, cols))
                        if k != 2:
                            for_magnitudes(i, ph, k)

            def search_rows(first, first_stored=None):
                for k in range(2):
                    if first_stored is not None:
                        sp.wait_ge(m_stored[k], first_stored)
                        alone(sp)
                    sp.dma_start(a_row[k], s_dram[first + k]).then_inc(s_full[k], 16)

            def again(first, k):
                sp.wait_ge(kill_ready, first + (k + 1))
                alone(sp)
                sp.dma_start(a_row[2], s_dram[first + k]).then_inc(s_again, 16)

            def mask_rows(first):
                for k in range(2):
                    again(first, k)

            for s in range(2):
                sp.wait_ge(stored[s], 16 * (NCH * NB // 2 + 1))
            sp.wait_ge(u_lo, 25)
            sp.wait_ge(mag_read, 24)
            sp.wait_ge(split_lo, 12)
            search_rows(0)
            with sp.Fori(0, 4) as i:
                chunk(i, 2)
                unit(i + 24, wd_a, i, IB * UW)
            mask_rows(0)
            search_rows(2, 16 * 2)
            with sp.Fori(0, 4) as i:
                unit(i + 28, wd_a, i + 4, IB * UW)
            again(2, 0)

            def masked_row(b, k):
                sp.wait_ge(m_stored[k], b * 16 + 48)
                alone(sp)
                if k:
                    sp.wait_ge(su_ready, b * BT + (BT + 1))
                else:
                    sp.wait_ge(m_ready, b * BT + (BT + (3 if isinstance(b, int) else 2)))
                alone(sp)
                sp.dma_start(a_row[2], m_dram[b * BT + (BT + k)]).then_inc(m_full, 16)

            def load_weights(b, *ns):
                for n in ns:
                    last = n - 2
                    g = last if last < 4 else 5 + 2 * (last - 4) if last < 12 else 8 + last
                    sp.wait_ge(mm_done[BT - 1], group(b, g + 1))
                    alone(sp)
                    src = wd_dram[n % 16 // 12] if n % 16 < 4 or n % 16 >= 12 else wgu_dram[(n - 4) // 4]
                    size = src.shape[-1]
                    sp.dma_start(W[:, n % 2, 0:2 * size].rearrange("p (u n) -> p u n", u=2),
                                 src[2 * (n % 4):2 * (n % 4) + 2].rearrange("u p n -> p u n"))\
                        .then_inc(w_full[n % 2], 16)

            masked_row(-1, 0)
            sp.wait_ge(stored[0], 16 * NCH * NB)
            for t in range(BT):
                if t == 1:
                    sp.wait_ge(u_lo, 33)
                if t == 2:
                    masked_row(-1, 1)
                    sp.wait_ge(u_stored, 16 * 33)
                sp.dma_start(S[:, t, 0:I], u_dram[t]).then_inc(row_full[t], 16)
            load_weights(0, 0)
            again(2, 1)
            for s in range(2):
                sp.wait_ge(stored[s], 16 * (NCH * NB + 1))

            def blocks(b, search):
                def weights(*ns):
                    load_weights(b, *ns)

                first = b * BT + BT
                weights(1)
                if search:
                    sp.wait_ge(su_ready, first)
                    alone(sp)
                    search_rows(first)
                for t in range(BT):
                    g = T_A[t] + 2
                    sp.wait_ge(tp_done[g % 2], (use(b - 1, g) if t < 2 else use(b, g)) + 1)
                    alone(sp)
                    sp.dma_start(S[:, t, 0:D], x_in[b * BT + t]).then_inc(row_full[t], 16)
                weights(2, 3, 4, 5, 6, 7)
                if search:
                    mask_rows(first)
                weights(8)
                if search:
                    search_rows(first + 2, b * 16 + 48)
                weights(9, 10, 11, 12, 13)
                if search:
                    sp.wait_ge(cand_ready[1], pair_base(b, 1, NBITS + 1, SLOTS + 1) + (TOP_STEPS + 1))
                    alone(sp)
                    masked_row(b, 0)
                    for t in range(BT):
                        g = T_H + 3 * t + 2
                        sp.wait_ge(tp_done[g % 2], use(b, g) + 1)
                        alone(sp)
                        sp.dma_start(S[:, t, 0:I], u_dram[first + t]).then_inc(row_full[t], 16)
                        if t == 1:
                            masked_row(b, 1)
                    sp.wait_ge(su_ready, first + 2)
                    alone(sp)
                    sp.dma_start(a_row[2], s_dram[first + 2]).then_inc(s_again, 16)
                weights(14)
                if search:
                    sp.wait_ge(us_ready, b * 2 + 1)
                    alone(sp)
                    sp.dma_start(a_row[2], s_dram[first + 3]).then_inc(s_again, 16)
                weights(15)
                if search:
                    weights(16)
                for t in range(BT):
                    sp.wait_ge(x1_stored, b * (16 * BT) + 16 * (t + 2))
                    alone(sp)
                    sp.wait_ge(out_ready, b * BT + (t + 1))
                    alone(sp)
                    sp.dma_start(x1_row, x1_dram[b * BT + t]).then_inc(x1_full, 16)

            for_blocks(sp, blocks)

        @block.gpsimd
        def _(pool):
            nc.gpsimd.memset(ident[:, :], 0.0).then_inc(pool_steps, 1)
            nc.gpsimd.memset(half[:, :], -0.5).then_inc(pool_steps, 1)
            pool.wait_ge(pool_steps, 2)
            nc.gpsimd.affine_select(out=ident[:, :], in_=ident[:, :], compare_op=ALU.not_equal, fill=1.0, base=0,
                                    pattern=[[-1, P]], channel_multiplier=1).then_inc(ident_ready, 1)
            pool.wait_ge(ident_ready, 1)
            for n, done in enumerate((u_stored, *stored, *m_stored, x1_stored, *out_stored)):
                pool.dma_start(first_dram[n], ident[:, 0:1]).then_inc(done, 16)

            def rstd(n, cols):
                pool.wait_ge(var_ready, n + 1)
                nc.gpsimd.tensor_tensor(rs[:, cols], mv[:, cols, 1], half[:, cols], ALU.pow).then_inc(rstd_ready, 1)

            def over_partitions(n, cols):
                pool.wait_ge(bounds_ready, n)
                nc.gpsimd.partition_all_reduce(gmx[:, cols], mx[:, 24 + cols.start:24 + cols.stop], P, RMAX)\
                    .then_inc(global_ready, 1)

            for n in range(4):
                rstd(n, slice(0, BT))
            over_partitions(1, slice(0, 4))
            def stage_out(ph, i, tq):
                dst, c = s_dram if ph < 2 else u_dram, i + 4 * (ph % 2)
                pool.wait_ge(bank_free[BT - 1], i * 4 + (16 * ph + tq + 2))
                alone(pool)
                pool.dma_start(dst[BT * tq:BT * (tq + 1)].rearrange("t p (c n) -> p t c n", c=NCH)[:, :, c, :],
                               stage[tq % 2]).then_inc(stored[tq % 2], 16)

            def unit_out(n, dst):
                pool.wait_ge(u_lo, n + 2)
                alone(pool)
                pool.dma_start(dst, raw(2, dst.shape[-1] // 2).bitcast(FP16)).then_inc(u_stored, 16)

            def masked_out(tile, k):
                pool.wait_ge(m_ready, tile + 1)
                alone(pool)
                pool.dma_start(m_dram[tile], a_row[k]).then_inc(m_stored[k], 16)

            for ph in range(2):
                with pool.Fori(0, 4) as i:
                    for tq in range(4):
                        stage_out(ph, i, tq)
                        if tq < 3:
                            unit_out(i * 3 + (12 * ph + tq), (*wgu_dram, wd_dram[1])[tq][i + 4 * ph])
                over_partitions(2 + ph, slice(4 + ph, 5 + ph))
            for ph in range(2, 4):
                def up_round(i, search):
                    for tq in range(4):
                        stage_out(ph, i, tq)
                        if tq == 1:
                            unit_out(i + (24 + 4 * (ph - 2)), wd_dram[0][i + 4 * (ph - 2)])
                        if not search and tq >= 2 and ph == 2:
                            masked_out(2 * (ph - 2) + (tq - 2), tq - 2)

                rounds(pool, up_round)

            def blocks(b, search):
                n = b * (3 * BT) + 4
                for t in range(BT):
                    rstd(n + 2 * t, slice(t, t + 1))
                    pool.wait_ge(x1_ready, b * BT + (t + 1))
                    alone(pool)
                    pool.dma_start(x1_dram[b * BT + t], Y[:, t, :]).then_inc(x1_stored, 16)
                    rstd(n + (2 * t + 1), slice(t, t + 1))
                if search:
                    for k in range(2):
                        masked_out(b * BT + (BT + k), k)
                for t in range(BT):
                    rstd(n + (2 * BT + t), slice(t, t + 1))
                    pool.wait_ge(out_ready, b * BT + (t + 2))
                    alone(pool)
                    pool.dma_start(out[b * BT + t], Y[:, t, :]).then_inc(out_stored[t], 16)

            for_blocks(pool, blocks)
            for t in range(BT):
                pool.wait_ge(out_stored[t], 16 * (NB + 1))

        @block.scalar
        def _(act):
            for u in range(BT):
                act.sem_inc(bank_free[u], 1)

            def high(slot, n_use, dst, n):
                act.wait_ge(tp_done[slot], n_use + 1)
                nc.scalar.activation(dst, tp(slot, n), ACT.Copy).then_inc(hi_done[slot], 1)

            def x_high(n):
                for t in range(BT * n, BT * (n + 1)):
                    high(t % 2, t // 2, flat(xT_a[:, t, 0, :, :]), KB)

            def split_high(place, src, m):
                nc.scalar.activation(wa[:, place, 0, :], src, ACT.Copy, scale=mul[:, m:m + 1]).then_inc(split_hi, 1)

            def magnitudes(at, src):
                nc.scalar.activation(JUNK[:, 1, 0:src.shape[-1]], src, ACT.Abs, accum_out=mx[:, at])\
                    .then_inc(mag_read, 1)

            for j in range(8):
                if j:
                    act.wait_ge(mag_read, j)
                act.wait_ge(mag_full[j % 4], 16 * (j // 4 + 1))
                magnitudes(slice(j, j + 1), raw(j % 4, KB * CW))
                if j in (1, 3, 5):
                    x_high((1, 3, 5).index(j))
            act.wait_ge(scales_ready, 1)
            for j in range(4):
                act.wait_ge(mag_full[j], 32)
                split_high(j, raw(j, KB * CW), AG)
                if j == 0:
                    x_high(3)

            def count(b, pair, j, summed=None):
                if summed is not None:
                    act.wait_ge(sum_ready, summed)
                act.wait_ge(cand_ready[0], pair_base(b, pair, NBITS + 1, SLOTS + 1) + j + 1)
                nc.scalar.activation(JUNK[:, 1, 0:I], a_row[0], ACT.Sign, scale=-1.0,
                                     bias=cand[:, 0:1].bitcast(FP32), accum_out=cnt[:, 0:1]).then_inc(act_count, 1)

            def evacuate(ph, i, tq, u):
                m = AG if ph < 2 else AU
                if u == 0:
                    act.wait_ge(stored[tq % 2], i * 32 + (16 * (8 * ph + tq // 2 + 1)))
                act.wait_ge(mm_done[u], i * 4 + (16 * ph + tq + 1))
                nc.scalar.activation(stage[tq % 2][:, u, :], PS[:, 4 + u, 0:CW], ACT.Silu if ph < 2 else ACT.Copy,
                                     scale=un[:, m:m + 1]).then_inc(bank_free[u], 1)

            def unit_high(n, width, src, mi):
                act.wait_ge(u_stored, n * 16 + 16)
                nc.scalar.activation(raw(2, width).bitcast(FP16)[:, 0:width], src, ACT.Copy,
                                     scale=mul[:, mi:mi + 1]).then_inc(u_hi, 1)

            def next_chunk(ph, i):
                act.wait_ge(chunk_full, i * 16 + (64 * ph + 16))
                alone(act)
                split_high(i, raw(0, KB * CW), AG if ph == 0 else AU)

            for ph in range(2):
                with act.Fori(0, 4) as i:
                    for tq in range(4):
                        for u in range(BT):
                            evacuate(ph, i, tq, u)
                        if tq < 3:
                            n, mi = i * 3 + (12 * ph + tq), UNITS[tq][-1]
                            width = KB * CW if mi != BD else IB * UW
                            act.wait_ge(w_ready, n + 2)
                            unit_high(n, width, raw(3, width), mi)
                        if tq < 2:
                            act.wait_ge(mag_next, i * 32 + (128 * ph + 16 * (tq + 1)))
                            act.wait_ge(mag_read, i * 2 + (8 * (ph + 1) + tq))
                            alone(act)
                            magnitudes(bass.ds(i * 2 + (8 * (ph + 1) + tq), 1),
                                       mag_row[:, 0:KB * CW if ph == 0 else IB * UW])
                    if ph == 1:
                        act.wait_ge(scales_ready, 2)
                    next_chunk(ph, i)
            def sum_of(b, t):
                if not isinstance(b, int) and t < 2:
                    act.wait_ge(act_count, pair_base(b, 1, NBITS, SLOTS) + (NBITS - 2 + t))
                elif t:
                    act.wait_ge(sum_ready, (b + 1) * (BT * NCH + BT) + t)
                act.wait_ge(su_ready, b * BT + (BT + t + 1))
                nc.scalar.activation(JUNK[:, 1, 0:I], S[:, t, 0:I], ACT.Abs, accum_out=hsum[:, t, 0:1])\
                    .then_inc(sum_ready, 1)

            def h_high(b, g0, t):
                for part, n in enumerate(TPARTS):
                    g = g0 + part
                    high(g % 2, use(b, g), flat(hT[:, t, 0, 8 * part:8 * part + n, :]), n)

            act.wait_ge(scales_ready, 3)
            for ph in range(2, 4):
                def up_round(i, search):
                    for tq in range(4):
                        for u in range(BT):
                            evacuate(ph, i, tq, u)
                            if not search and ph == 3 and (tq, u) in ((2, 3), (3, 1)):
                                sum_of(-1, tq - 2)
                            at = u - (BT - UP_STEPS[tq])
                            if search and at >= 0:
                                count(None, ph - 2, i * sum(UP_STEPS) + (sum(UP_STEPS[:tq]) + at))
                        if tq == 1:
                            n = i + (24 + 4 * (ph - 2))
                            act.wait_ge(unit_full, n * 16 + 16)
                            unit_high(n, IB * UW, raw(1, IB * UW), AD)
                    if ph == 2:
                        next_chunk(ph, i)

                rounds(act, up_round)

            for t in range(2):
                h_high(-1, T_A[t], t)
            sum_of(-1, 2)
            sum_of(-1, 3)
            for s in range(2):
                act.wait_ge(stored[s], 16 * (NCH * NB + 1))

            def blocks(b, search):
                def x_high_b(t):
                    high(t % 2, use(b, T_X + t), flat(xT_b[:, t, 0, :, :]), KB)

                def y_rows(g0, layer, c, t):
                    if layer == 0 and c == 0:
                        act.wait_ge(out_stored[t], b * 16 + 16)
                    act.wait_ge(mm_done[t], group(b, g0 + c) + 1)
                    nc.scalar.activation(Y[:, t, 2 * UW * c:2 * UW * (c + 1)], PS[:, 4 + t, 0:2 * UW], ACT.Copy,
                                         scale=inv[:, layer, t:t + 1]).then_inc(bank_free[t], 1)

                def silu(c, t):
                    act.wait_ge(mm_done[t], group(b, G_GATE + c) + 1)
                    nc.scalar.activation(S[:, t, c * CW:(c + 1) * CW], PS[:, 4 + t, 0:CW], ACT.Silu,
                                         scale=un[:, BG:BG + 1]).then_inc(bank_free[t], 1)

                def counts(pair, j, n):
                    for k in range(n):
                        if search:
                            count(b, pair, j + k)
                    return j + n

                def sum_b(c, t):
                    act.wait_ge(bank_free[t], group(b, G_UP + c) + 2)
                    nc.scalar.activation(junk_b[:, c, t, :], S[:, t, c * CW:(c + 1) * CW], ACT.Abs,
                                         accum_out=hsum[:, t, c:c + 1]).then_inc(sum_ready, 1)

                j = 0
                for c in range(4):
                    for t in range(BT):
                        y_rows(0, 0, c, t)
                        if c == 0 and t < 2:
                            h_high(b, T_A[t + 2], t + 2)
                        if c == 3 and t >= 2:
                            x_high_b(t - 2)
                        j = counts(0, j, DOWN_A_STEPS[c][t])
                for c in range(NCH):
                    for t in range(BT):
                        silu(c, t)
                        if c == 0 and t < 2:
                            x_high_b(t + 2)
                        j = counts(0, j, GATE_STEPS[c][t])
                j = 0
                for c in range(NCH):
                    for t in range(BT):
                        j = counts(1, j, UP_B_STEPS[c][t])
                        sum_b(c, t)
                h_high(b, T_H, 0)
                h_high(b, T_H + 3, 1)
                act.wait_ge(x1_stored, b * (16 * BT) + 16 * (BT + 1))
                for c in range(4):
                    for t in range(BT):
                        y_rows(G_DOWN, 1, c, t)
                        if c == 0 and t < 2:
                            h_high(b, T_H + 3 * (t + 2), t + 2)
                        if search and (c, t) in DOWN_B_STEPS_AT:
                            n = DOWN_B_STEPS_AT.index((c, t))
                            count(b, 1, j, (b + 1) * (BT * NCH + BT) + n if n else None)
                            j += 1
                        if search and (c, t) in SUMS_AT:
                            sum_of(b, SUMS_AT.index((c, t)))
                        if search and c == 3 and 1 <= t <= 2:
                            h_high(b, T_A[t - 1], t - 1)

            for_blocks(act, blocks)

        @block.vector
        def _(dve):
            step = Steps(dve_steps)

            def then(ins, apart=False):
                dve.wait_ge(dve_steps, step.add(ins))
                if apart:
                    alone(dve)

            dve.sem_inc(u_lo, 1)
            dve.sem_inc(w_ready, 1)
            dve.sem_inc(lo_done[0], 1)
            dve.sem_inc(lo_done[1], 1)
            dve.sem_inc(out_ready, 1)
            for j in range(SLOTS):
                nc.vector.memset(bitf[:, j:j + 1], float(2 ** (NBITS - 1 - j)) if j < NBITS else 0.0)
                nc.vector.memset(bitn[:, j:j + 1], 2 ** (NBITS - 2 - j) if j < NBITS - 1 else 0)
            nc.vector.memset(hsum[:, :, :], TINY)
            then(nc.vector.memset(mx[:, 24:30], 0.0))

            def scales(n, first, matrix, cols, x_cols):
                dve.wait_ge(mag_read, first + 8)
                nc.vector.tensor_reduce(out=mx[:, 24 + matrix:25 + matrix], in_=mx[:, first:first + 8], op=ALU.max,
                                        axis=AX.X).then_inc(bounds_ready, 1)
                dve.wait_ge(global_ready, n)
                g = gmx[:, cols]
                then(nc.vector.tensor_scalar(g, g, TINY, None, ALU.max))
                then(nc.vector.tensor_scalar(g.bitcast(INT32), g.bitcast(INT32), EXP_BITS, None, ALU.bitwise_and))
                then(nc.vector.reciprocal(mul[:, cols], g))
                then(nc.vector.tensor_scalar(un[:, cols], g, 1.0 / TOP, None, ALU.mult))
                if x_cols:
                    then(nc.vector.tensor_scalar(un[:, x_cols], un[:, x_cols], 1.0 / XS, None, ALU.mult))
                nc.vector.tensor_scalar(mul[:, cols], mul[:, cols], TOP, None, ALU.mult).then_inc(scales_ready, 1)
                dve.wait_ge(scales_ready, n)

            def statistics(rows, t):
                h = D // 2
                nc.vector.bn_stats(st[:, t, 0:6], rows[:, 0:h])
                return nc.vector.bn_stats(st[:, t, 6:12], rows[:, h:D])

            def low(slot, n_use, dst, hi, n):
                dve.wait_ge(hi_done[slot], n_use + 1)
                nc.vector.tensor_tensor(dst, tp(slot, n), hi, ALU.subtract).then_inc(lo_done[slot], 1)

            def normalised(n):
                x = x_place[n]
                dve.wait_ge(x_full[n], 16)
                for t in range(BT):
                    last = statistics(x[:, t, :], t)
                then(last)
                for t in range(BT):
                    last = nc.vector.bn_aggr(mv[:, t, :], st[:, t, :])
                then(last)
                nc.vector.tensor_scalar(mv[:, :, 1], mv[:, :, 1], EPS, None, ALU.add).then_inc(var_ready, 1)
                dve.wait_ge(rstd_ready, n + 1)
                then(nc.vector.tensor_scalar(rx[:, :], rs[:, :], XS, None, ALU.mult))
                for t in range(BT):
                    nc.vector.tensor_scalar(x[:, t, :], x[:, t, :], mv[:, t, 0:1], rx[:, t:t + 1], ALU.subtract,
                                            ALU.mult).then_inc(xs_ready, 1)

            def x_low(n):
                for t in range(BT * n, BT * (n + 1)):
                    low(t % 2, t // 2, flat(xT_a[:, t, 1, :, :]), flat(xT_a[:, t, 0, :, :]), KB)

            def split_low(n, place, src, m):
                dve.wait_ge(split_hi, n + 1)
                nc.vector.scalar_tensor_tensor(out=wa[:, place, 1, :], in0=src, scalar=mul[:, m:m + 1],
                                               in1=wa[:, place, 0, :], op0=ALU.mult, op1=ALU.subtract)\
                    .then_inc(split_lo, 1)

            normalised(0)
            normalised(1)
            x_low(0)
            normalised(2)
            x_low(1)
            dve.wait_ge(zs_full, 96)
            for n, (_, _, rows, cols) in enumerate(BOUNDS):
                z, s = (a[0:rows, 0:cols] for a in bounds_in[n])
                then(nc.vector.tensor_scalar(z.bitcast(INT32), z.bitcast(INT32), ABS_BITS, None, ALU.bitwise_and))
                then(nc.vector.scalar_tensor_tensor(out=z, in0=z, scalar=15.0, in1=s, op0=ALU.add, op1=ALU.mult))
                at = 24 + (BG, BU, BD)[n]
                then(nc.vector.tensor_reduce(out=mx[0:rows, at:at + 1], in_=z, op=ALU.max, axis=AX.X,
                                             apply_absolute_value=True))

            x_low(2)
            normalised(3)
            scales(1, 0, AG, slice(0, 4), slice(0, 3))
            split_low(0, 0, raw(0, KB * CW), AG)
            x_low(3)
            for j in range(1, 4):
                split_low(j, j, raw(j, KB * CW), AG)
            dve.wait_ge(split_lo, 4)

            def dequantise(n, k, width, blocks):
                q = raw(1, blocks * width).bitcast(INT32).rearrange("p (j n) -> p j n", j=blocks)
                w = raw(3, 2 * blocks * width)
                w4 = w.rearrange("p (j e n) -> p j e n", j=blocks, e=2)
                wi = w.bitcast(INT32).rearrange("p (j e n) -> p j e n", j=blocks, e=2)
                dve.wait_ge(unit_full, n * 16 + 16)
                nc.vector.tensor_scalar(wi[:, :, 0, :], q, 4, 15, ALU.logical_shift_right, ALU.bitwise_and)
                then(nc.vector.tensor_scalar(wi[:, :, 1, :], q, 15, None, ALU.bitwise_and))
                dve.wait_ge(unit_zs, n * 32 + 32)
                if k < 2:
                    z, s = (a_row[d][:, 0:width].unsqueeze(1).to_broadcast([P, 2 * blocks, width]) for d in range(2))
                    w4, wi = (a.rearrange("p j e n -> p (j e) n") for a in (w4, wi))
                else:
                    z, s = (a_row[d][:, 0:blocks * width].rearrange("p (j n) -> p j n", j=blocks).unsqueeze(2)
                            .to_broadcast([P, blocks, 2, width]) for d in range(2))
                then(nc.vector.tensor_tensor(w4, wi, z, ALU.subtract))
                nc.vector.tensor_tensor(w4, w4, s, ALU.mult).then_inc(w_ready, 1)
                return w

            def unit_low(n, w, mi):
                width = w.shape[-1]
                hl = raw(2, width).bitcast(FP16)
                dve.wait_ge(u_hi, n + 1)
                nc.vector.scalar_tensor_tensor(out=hl[:, width:2 * width], in0=w, scalar=mul[:, mi:mi + 1],
                                               in1=hl[:, 0:width], op0=ALU.mult, op1=ALU.subtract).then_inc(u_lo, 1)

            for ph in range(2):
                with dve.Fori(0, 4) as i:
                    kept = step.enter(i, 6)
                    for k, (_, _, _, _, _, mi) in enumerate(UNITS):
                        n = i * 3 + (12 * ph + k)
                        dve.wait_ge(u_lo, n + 1)
                        w = dequantise(n, k, CW if k < 2 else UW, KB // 2 if k < 2 else JB)
                        unit_low(n, w, mi)
                    split_low(i + 4 * (ph + 1), i, raw(0, KB * CW), AG if ph == 0 else AU)
                    step.leave(kept, 4)
                scales(2 + ph, 8 * (ph + 1), AU + ph, slice(4 + ph, 5 + ph), slice(4, 5) if ph == 0 else None)

            def start_pair(b, pair, n_full):
                if b is not None:
                    dve.wait_ge(s_full[1], n_full)
                    halves = a_row[1].bitcast(INT16).rearrange("p (n two) -> p two n", two=2)
                    taken = step.add(nc.vector.tensor_scalar(upper.bitcast(INT16), halves[:, 1, :], 0x7FFF, None,
                                                             ALU.bitwise_and))
                for k in range(2):
                    dve.wait_ge(s_full[k], n_full)
                    if b is not None and k:
                        dve.wait_ge(dve_steps, taken)
                    a = a_row[k].bitcast(INT32)
                    nc.vector.tensor_scalar(a, a, ABS_BITS, None, ALU.bitwise_and)
                for k in range(2):
                    nc.vector.memset(cand[:, k:k + 1], 2 ** (NBITS - 1)).then_inc(cand_ready[k], 1)

            def search_step(b, pair, j, beside=None):
                base = pair_base(b, pair, NBITS + 1, SLOTS + 1)
                bit, nxt = bitf[:, bass.ds(j, 1)], bitn[:, bass.ds(j, 1)]
                dve.wait_ge(cand_ready[1], base + j + 1)
                top = isinstance(j, int) and j < TOP_STEPS
                second = step.add(nc.vector.tensor_scalar(upper_junk if top else JUNK[:, 0, 0:I],
                                                          upper if top else a_row[1], cand[:, 1:2].bitcast(FP32), None,
                                                          ALU.is_lt, ALU.add, accum_out=cnt[:, 1:2]))
                if beside:
                    beside()
                dve.wait_ge(act_count, pair_base(b, pair, NBITS, SLOTS) + j + 1)
                flipped = [step.add(nc.vector.tensor_scalar(flip[:, 0:1], cnt[:, 0:1], 0.0, bit,
                                                            ALU.is_ge, ALU.mult))]
                dve.wait_ge(dve_steps, second)
                flipped.append(step.add(nc.vector.tensor_scalar(flip[:, 1:2], cnt[:, 1:2], DROPPED - 0.5, bit,
                                                                ALU.is_ge, ALU.mult)))
                for k in range(2):
                    dve.wait_ge(dve_steps, flipped[k])
                    nc.vector.scalar_tensor_tensor(out=cand[:, k:k + 1], in0=cand[:, k:k + 1],
                                                   scalar=flip[:, k:k + 1], in1=nxt, op0=ALU.bitwise_xor,
                                                   op1=ALU.bitwise_xor).then_inc(cand_ready[k], 1)

            def threshold(b, pair, k):
                T = cand[:, k:k + 1]
                a = a_row[k]
                dve.wait_ge(cand_ready[k], (pair_base(b, pair, NBITS + 1, SLOTS + 1) + NBITS + 1) if b is not None
                            else (SLOTS + 1) * (pair + 1))
                then(nc.vector.tensor_scalar(JUNK[:, 0, 0:I], a, T.bitcast(FP32), None, ALU.is_le, ALU.add,
                                             accum_out=cnt[:, k:k + 1]))
                nc.vector.tensor_scalar(fin[:, k:k + 1], cnt[:, k:k + 1], DROPPED - 0.5, None, ALU.is_ge)
                then(nc.vector.tensor_scalar(flip[:, k:k + 1], cnt[:, k:k + 1], DROPPED - 0.5, None, ALU.is_le),
                     apart=True)
                then(nc.vector.tensor_tensor(T, T, flip[:, k:k + 1], ALU.add))
                then(nc.vector.tensor_scalar(JUNK[:, 0, 0:I], a, T.bitcast(FP32), None, ALU.is_equal))

            def ties(k, n_kill):
                then(nc.vector.tensor_tensor_scan(a_row[2], JUNK[:, 0, 0:I], JUNK[:, 0, 0:I], 0.0, ALU.add, ALU.bypass))
                then(nc.vector.tensor_tensor(fin[:, k:k + 1], fin[:, k:k + 1], a_row[2][:, I - 1:I], ALU.mult))
                then(nc.vector.tensor_tensor(fin[:, k:k + 1], fin[:, k:k + 1], cnt[:, k:k + 1], ALU.subtract))
                then(nc.vector.tensor_scalar(fin[:, k:k + 1], fin[:, k:k + 1], float(DROPPED), None, ALU.add))
                nc.vector.scalar_tensor_tensor(out=JUNK[:, 0, 0:I], in0=a_row[2], scalar=fin[:, k:k + 1],
                                               in1=JUNK[:, 0, 0:I], op0=ALU.is_le, op1=ALU.mult).then_inc(kill_ready, 1)
                dve.wait_ge(kill_ready, n_kill)

            def masked(k, n_again):
                a = a_row[k]
                kept = nc.vector.scalar_tensor_tensor(out=a, in0=a, scalar=cand[:, k:k + 1].bitcast(FP32),
                                                      in1=JUNK[:, 0, 0:I], op0=ALU.is_ge, op1=ALU.subtract)
                if n_again is None:
                    kept.then_inc(m_ready, 1)
                    return
                then(kept)
                dve.wait_ge(s_again, n_again * 16)
                nc.vector.tensor_tensor(a, a, a_row[2], ALU.mult).then_inc(m_ready, 1)

            def mask(b, pair, k):
                first = 2 * pair if b is None else b * BT + (BT + 2 * pair)
                if k:
                    dve.wait_ge(m_ready, first + k)
                threshold(b, pair, k)
                ties(k, first + (k + 1))
                masked(k, None if b is not None and pair else first + (k + 1))

            def scales_of(tiles, sums):
                a = hs[:, 0, tiles]
                then(nc.vector.tensor_reduce(out=a, in_=sums, op=ALU.add, axis=AX.X))
                then(nc.vector.reciprocal(a, a))
                then(nc.vector.tensor_scalar(a.bitcast(INT32), a.bitcast(INT32), EXP_BITS, None, ALU.bitwise_and))

            def scaled(t, ready):
                rows = S[:, t, 0:I]
                nc.vector.tensor_scalar(rows, rows, hs[:, 0, t:t + 1], H_TOP, ALU.mult, ALU.mult).then_inc(ready, 1)

            def unscales_of(tiles, layer, matrix):
                then(nc.vector.reciprocal(hs[:, 1, tiles], hs[:, 0, tiles]))
                then(nc.vector.tensor_scalar(inv[:, layer, tiles], hs[:, 1, tiles], 1.0 / H_TOP,
                                             un[:, matrix:matrix + 1], ALU.mult, ALU.mult))

            def su_product(b, t):
                rows = S[:, t, 0:I]
                if t < 2:
                    dve.wait_ge(m_full, b * 32 + (48 + 16 * t))
                else:
                    dve.wait_ge(m_ready, b * BT + (BT + t + 1))
                dve.wait_ge(row_full[t], b * 32 + 48)
                nc.vector.tensor_tensor(rows, rows, a_row[2 if t < 2 else t - 2], ALU.mult).then_inc(su_ready, 1)

            def us_product(b, t):
                rows = S[:, t, 0:I]
                dve.wait_ge(row_full[t], b * 32 + 48)
                dve.wait_ge(s_again, b * (16 * BT) + 16 * (BT + t + 1))
                nc.vector.tensor_tensor(rows, rows, a_row[2], ALU.mult).then_inc(us_ready, 1)

            def su_scale(b, t):
                dve.wait_ge(sum_ready, (b + 1) * (BT * NCH + BT) + (t + 1))
                scales_of(slice(t, t + 1), hsum[:, t, 0:NCH + 1:NCH])
                scaled(t, h_ready)
                unscales_of(slice(t, t + 1), 0, AD)

            def h_low(b, g0, t):
                for part, n in enumerate(TPARTS):
                    g = g0 + part
                    low(g % 2, use(b, g), flat(hT[:, t, 1, 8 * part:8 * part + n, :]),
                        flat(hT[:, t, 0, 8 * part:8 * part + n, :]), n)

            for ph in range(2, 4):
                start_pair(None, ph - 2, 16 * (ph - 1))

                def up_round(i, search):
                    n = i + (24 + 4 * (ph - 2))
                    if search:
                        kept = step.enter(i, 3 * sum(UP_STEPS))
                        for k in range(sum(UP_STEPS)):
                            search_step(None, ph - 2, i * sum(UP_STEPS) + k)
                            if k == sum(UP_STEPS[:2]) - 1:
                                unit_low(n, raw(1, IB * UW), AD)
                    else:
                        mask(None, ph - 2, 0)
                        unit_low(n, raw(1, IB * UW), AD)
                        if ph == 2:
                            mask(None, 0, 1)
                            split_low(15, 3, raw(0, KB * CW), AU)
                            return
                        for t in range(2):
                            su_product(-1, t)
                            su_scale(-1, t)
                        dve.wait_ge(m_ready, 3)
                        threshold(None, 1, 1)
                        ties(1, 4)
                        h_low(-1, T_A[0], 0)
                        masked(1, 4)
                        h_low(-1, T_A[1], 1)
                        return
                    if ph == 2:
                        split_low(i + 12, i, raw(0, KB * CW), AU)
                    if search:
                        step.leave(kept, 3)

                rounds(dve, up_round)
            for t in range(2, BT):
                su_product(-1, t)
                su_scale(-1, t)

            def blocks(b, search):
                def x_low_b(t):
                    low(t % 2, use(b, T_X + t), flat(xT_b[:, t, 1, :, :]), flat(xT_b[:, t, 0, :, :]), KB)

                def mean_rstd(t, n):
                    then(statistics(Y[:, t, :], t), apart=True)
                    then(nc.vector.bn_aggr(mv[:, t, :], st[:, t, :]))
                    nc.vector.tensor_scalar(mv[:, t, 1:2], mv[:, t, 1:2], EPS, None, ALU.add).then_inc(var_ready, 1)
                    dve.wait_ge(rstd_ready, b * (3 * BT) + (4 + n + 1))

                def normalise(t):
                    y = Y[:, t, :]
                    then(nc.vector.tensor_scalar(y, y, mv[:, t, 0:1], rs[:, t:t + 1], ALU.subtract, ALU.mult))

                def x1(t):
                    y = Y[:, t, :]
                    dve.wait_ge(bank_free[t], group(b, 3) + 2)
                    mean_rstd(t, 2 * t)
                    normalise(t)
                    dve.wait_ge(row_full[t], b * 32 + 32)
                    nc.vector.tensor_tensor(y, y, S[:, t, 0:D], ALU.add).then_inc(x1_ready, 1)
                    dve.wait_ge(x1_ready, b * BT + (t + 1))
                    mean_rstd(t, 2 * t + 1)
                    then(nc.vector.tensor_scalar(rx[:, t:t + 1], rs[:, t:t + 1], XS, None, ALU.mult))
                    nc.vector.tensor_scalar(S[:, t, D:2 * D], y, mv[:, t, 0:1], rx[:, t:t + 1], ALU.subtract,
                                            ALU.mult).then_inc(xs_ready, 1)

                def out_rows(t):
                    y = Y[:, t, :]
                    dve.wait_ge(bank_free[t], group(b, G_PER - 1) + 2)
                    mean_rstd(t, 2 * BT + t)
                    normalise(t)
                    dve.wait_ge(x1_full, b * (16 * BT) + 16 * (t + 1))
                    nc.vector.tensor_tensor(y, y, x1_row, ALU.add).then_inc(out_ready, 1)

                def steps(pair, j, n):
                    for k in range(n):
                        if search:
                            search_step(b, pair, j + k)
                    return j + n

                def times_s(c, t):
                    dve.wait_ge(mm_done[t], group(b, G_UP + c) + 1)
                    rows = S[:, t, c * CW:(c + 1) * CW]
                    nc.vector.scalar_tensor_tensor(out=rows, in0=PS[:, 4 + t, 0:CW], scalar=un[:, BU:BU + 1],
                                                   in1=rows, op0=ALU.mult, op1=ALU.mult).then_inc(bank_free[t], 1)

                per = BT * 6 + 5 + BT * 3
                if search:
                    per += 2 * (3 * NBITS + 1) + BT * 9 - 2 + BT * 5
                kept = step.enter(b, per) if search else None
                h_low(b, T_A[2], 2)
                h_low(b, T_A[3], 3)
                if search:
                    start_pair(b, 0, b * 32 + 48)
                j = 0
                for c in range(3):
                    j = steps(0, j, sum(DOWN_A_STEPS[c]))
                x1(0)
                x1(1)
                x1(2)
                x_low_b(0)
                x1(3)
                for t in range(1, BT):
                    x_low_b(t)
                for c in range(NCH):
                    j = steps(0, j, sum(GATE_STEPS[c]))
                if search:
                    mask(b, 0, 0)
                    mask(b, 0, 1)
                    start_pair(b, 1, b * 32 + 64)
                j = 0
                for c in range(NCH):
                    for t in range(BT):
                        if search and UP_B_STEPS[c][t]:
                            search_step(b, 1, j, lambda: times_s(c, t))
                            j += 1
                        else:
                            times_s(c, t)
                dve.wait_ge(sum_ready, (b + 1) * (BT * NCH + BT))
                scales_of(slice(0, BT), hsum[:, :, :])
                for t in range(BT):
                    scaled(t, hb_ready)
                    if t == 1:
                        unscales_of(slice(0, BT), 1, BD)
                    if t:
                        h_low(b, T_H + 3 * (t - 1), t - 1)
                h_low(b, T_H + 3 * (BT - 1), BT - 1)
                if search:
                    su_product(b, 0)
                    j = steps(1, j, 1)
                    su_product(b, 1)
                    su_scale(b, 0)
                    j = steps(1, j, 1)
                    us_product(b, 2)
                    su_scale(b, 1)
                    j = steps(1, j, 1)
                    us_product(b, 3)
                    dve.wait_ge(us_ready, b * 2 + 2)
                    mask(b, 1, 0)
                    su_product(b, 2)
                    mask(b, 1, 1)
                    su_product(b, 3)
                    su_scale(b, 2)
                    su_scale(b, 3)
                for t in range(BT):
                    out_rows(t)
                    if search and t < 2:
                        h_low(b, T_A[t], t)
                if search:
                    step.leave(kept, NB - 1)

            for_blocks(dve, blocks)

        @block.tensor
        def _(pe):
            def transposes(slot, n_use, source, n):
                pe.wait_ge(lo_done[slot], n_use + 1)
                for k in range(n):
                    rows = source(k)
                    m = rows.shape[-1]
                    last = nc.tensor.transpose(tp(slot, n)[0:m, k * P:(k + 1) * P], rows, ident[:, :])
                last.then_inc(tp_done[slot], 1)

            def products(bank, lhs, rhs, blocks, width, rows_last=P):
                n = 0
                for kb in range(blocks):
                    m = rows_last if kb >= blocks - 2 else P
                    for hx, hw in ((0, 0), (0, 1), (1, 0)):
                        last = nc.tensor.matmul(PS[:, 4 + bank, 0:width], lhs(hx, kb, m), rhs(hw, kb, m),
                                                start=n == 0, stop=n == 3 * blocks - 1)
                        n += 1
                last.then_inc(mm_done[bank], 1)

            pe.wait_ge(ident_ready, 1)
            for n in range(4):
                for u in range(BT):
                    t = BT * n + u
                    rows = x_place[n][:, u, :].rearrange("p (a k) -> p k a", k=KB)
                    pe.wait_ge(xs_ready, t + 1)
                    transposes(t % 2, t // 2, lambda k: rows[:, k, :], KB)
            for s in range(2):
                pe.wait_ge(lo_done[s], NT // 2 + 1)
            with pe.Fori(0, 4) as ph:
                with pe.Fori(0, 4) as i:
                    pe.wait_ge(split_lo, ph * 4 + i + 1)
                    alone(pe)
                    with pe.Fori(0, NT // BT) as tq:
                        for u in range(BT):
                            pe.wait_ge(bank_free[u], ph * 16 + i * 4 + tq + 1)
                            products(u, lambda h, kb, m: xT_a[:, tq * BT + u, h, kb, :],
                                     lambda h, kb, m: wa[:, i, h, kb * CW:(kb + 1) * CW], KB, CW)

            def h_transposed(b, g0, ready, n_ready, t):
                pe.wait_ge(ready, n_ready)
                alone(pe)
                rows = S[:, t, :].rearrange("p (j m e) -> p j e m", j=JB, e=2)
                for part, n in enumerate(TPARTS):
                    g = g0 + part

                    def block_rows(k):
                        kb = 8 * part + k
                        return rows[:, kb // 2, kb % 2, 0:PL if kb >= IB - 2 else P]

                    transposes(g % 2, use(b, g), block_rows, n)

            for t in range(2):
                h_transposed(-1, T_A[t], h_ready, t + 1, t)

            def blocks(b, search):
                def split(b, g):
                    pe.wait_ge(lo_done[g % 2], use(b, g) + 2)

                def down(g0, n0, c, t):
                    n = n0 + c
                    if t == 0:
                        pe.wait_ge(w_full[n % 2], b * 128 + 16 * (n // 2 + 1))
                        alone(pe)
                    pe.wait_ge(bank_free[t], group(b, g0 + c) + 1)
                    products(t, lambda h, kb, m: hT[0:m, t, h, kb, :],
                             lambda h, kb, m: w_down[n % 2][0:m, :, h, kb, :], IB, 2 * UW, PL)

                def gate_up(g0, n0, c, t):
                    n = n0 + c // 2
                    if t == 0 and c % 2 == 0:
                        pe.wait_ge(w_full[n % 2], b * 128 + 16 * (n // 2 + 1))
                        alone(pe)
                    pe.wait_ge(bank_free[t], group(b, g0 + c) + 1)
                    products(t, lambda h, kb, m: xT_b[:, t, h, kb, :],
                             lambda h, kb, m: w_gu(n % 2, c % 2)[:, h, kb, :], KB, CW)

                def h_split(b, g0):
                    split(b, g0 + 1)
                    split(b, g0 + 2)

                def x_transposed(t):
                    pe.wait_ge(xs_ready, b * BT + (NT + t + 1))
                    alone(pe)
                    rows = S[:, t, D:2 * D].rearrange("p (a k) -> p k a", k=KB)
                    transposes(t % 2, use(b, T_X + t), lambda k: rows[:, k, :], KB)

                for c in range(4):
                    for t in range(BT):
                        if c == 0:
                            h_split(b - 1 if t < 2 else b, T_A[t])
                        down(0, 0, c, t)
                        if c == 0 and t < 2:
                            h_transposed(b, T_A[t + 2], h_ready, b * BT + (t + 3), t + 2)
                        if c == 3 and t >= 2:
                            x_transposed(t - 2)
                for c in range(2 * NCH):
                    for t in range(BT):
                        if c == 0:
                            split(b, T_X + t)
                        gate_up(G_GATE, 4, c, t)
                        if c == 0 and t < 2:
                            x_transposed(t + 2)
                h_transposed(b, T_H, hb_ready, b * BT + 1, 0)
                h_transposed(b, T_H + 3, hb_ready, b * BT + 2, 1)
                for c in range(4):
                    for t in range(BT):
                        if c == 0:
                            h_split(b, T_H + 3 * t)
                        down(G_DOWN, 12, c, t)
                        if c == 0 and t < 2:
                            h_transposed(b, T_H + 3 * (t + 2), hb_ready, b * BT + (t + 3), t + 2)
                        if search and c == 3 and 1 <= t <= 2:
                            h_transposed(b, T_A[t - 1], h_ready, b * BT + (BT + t), t - 1)

            for_blocks(pe, blocks)


_NAMES = ["x", "wg_a", "wu_a", "wd_a", "qg", "qu", "qd", "sg", "zg", "su", "zu", "sd", "zd"]


def kernel(L0_attn_x, L0_attn_w_gate, L0_attn_w_up, L0_attn_w_down, L0_ffn_gate_Wq, L0_ffn_up_Wq, L0_ffn_down_Wq,
           L0_ffn_gate_scale, L0_ffn_gate_zero, L0_ffn_up_scale, L0_ffn_up_zero, L0_ffn_down_scale, L0_ffn_down_zero):
    import numpy as np
    import concourse.bacc as bacc
    from concourse.bass_utils import run_bass_kernel_spmd

    def contraction_chunks(w):
        w = np.asarray(w).T
        return w.reshape(P, w.shape[0] // P, NCH, CW).transpose(2, 0, 1, 3)

    def group_chunks(a):
        a = np.asarray(a).T
        return a.reshape(a.shape[0], NCH, CW).transpose(1, 0, 2)

    def padded(w, rows):
        w = np.asarray(w).T
        return np.concatenate([w, np.zeros((rows - w.shape[0], w.shape[1]), w.dtype)])

    def down_units(w):
        w = padded(w, IB * P).reshape(JB, P, 2, NU, UW)
        return w.transpose(3, 1, 0, 2, 4).reshape(NU, P, IB * UW)

    def packed_units(w):
        w = padded(w, JB * P).reshape(JB, P, NU, UW)
        return w.transpose(2, 1, 0, 3).reshape(NU, P, JB * UW)

    def group_units(a):
        a = padded(a, JB * 4).reshape(JB, 4, NU, UW)
        return a.transpose(2, 1, 0, 3).reshape(NU, 4, JB * UW)

    arrays = {
        "x": np.asarray(L0_attn_x).reshape(NT, P, D),
        "wg_a": contraction_chunks(L0_attn_w_gate).reshape(NCH, P, KB * CW),
        "wu_a": contraction_chunks(L0_attn_w_up).reshape(NCH, P, KB * CW),
        "wd_a": down_units(L0_attn_w_down),
        "qg": contraction_chunks(L0_ffn_gate_Wq).reshape(NCH, P, KB // 2 * CW),
        "qu": contraction_chunks(L0_ffn_up_Wq).reshape(NCH, P, KB // 2 * CW),
        "qd": packed_units(L0_ffn_down_Wq),
        "sg": group_chunks(L0_ffn_gate_scale), "zg": group_chunks(L0_ffn_gate_zero),
        "su": group_chunks(L0_ffn_up_scale), "zu": group_chunks(L0_ffn_up_zero),
        "sd": group_units(L0_ffn_down_scale), "zd": group_units(L0_ffn_down_zero),
    }
    arrays = {n: np.ascontiguousarray(a) for n, a in arrays.items()}
    nc = bacc.Bacc("TRN2", target_bir_lowering=False, num_devices=1)
    args = [nc.dram_tensor(f"in_{n}", arrays[n].shape, mybir.dt.from_np(arrays[n].dtype), kind="ExternalInput").ap()
            for n in _NAMES]
    out = nc.dram_tensor("out", (NT, P, D), FP32, kind="ExternalOutput").ap()
    build(nc, *args, out)
    r = run_bass_kernel_spmd(nc, [{f"in_{n}": arrays[n] for n in _NAMES}], core_ids=[0])
    return r.results[0]["out"].reshape(1, TOKENS, D)
```
